# Optimizing a Trainium2 kernel written in Bass

```python
import numpy as np
import jax
import jax.numpy as jnp

def _softmax(x, axis=-1):
    return jax.nn.softmax(x, axis=axis)

def _gelu(x):
    return jax.nn.gelu(x, approximate=True)

def _silu(x):
    return jax.nn.silu(x)

def _sigmoid(x):
    return jax.nn.sigmoid(x)

def _layernorm(x, axis=-1, eps=1e-05):
    m = jnp.mean(x, axis=axis, keepdims=True)
    v = jnp.var(x, axis=axis, keepdims=True)
    return (x - m) / jnp.sqrt(v + eps)

def _scatter_add(tgt, idx, src, axis=0):
    return tgt.at[idx].add(src)

def _segment_sum(src, seg, n):
    return jax.ops.segment_sum(src, seg, n)
kernel_name = 'mk_xattn_ffn_d1_seqx_r4_667386'

def setup_inputs(seed: int=0):
    np.random.seed(seed)
    _w = jnp.asarray

    def _rec_inputs():
        import jax
        import jax.numpy as jnp
        _rk = jax.random.key(seed)
        x = 7.22e-05 + 1 * jax.random.normal(jax.random.fold_in(_rk, 1), (64, 256, 256), jnp.float32)
        _lenS = 256 - jax.random.randint(jax.random.fold_in(_rk, 7), (64,), 0, max(1, 256 // 4) + 1, jnp.int32)
        _lenS2 = 77 - jax.random.randint(jax.random.fold_in(_rk, 8), (64,), 0, max(1, 77 // 4) + 1, jnp.int32)
        _ctx_768P = jax.random.normal(jax.random.fold_in(_rk, 11), (64, 16, 192), jnp.float32)
        _ctx_768c = jax.random.dirichlet(jax.random.fold_in(_rk, 511), 0.3 * jnp.ones((16,), jnp.float32), (64, 77))
        _ctx_768t = jnp.einsum('bsk,bkd->bsd', _ctx_768c, _ctx_768P)
        _ctx_768t = _ctx_768t * jax.lax.rsqrt(jnp.mean(jnp.square(_ctx_768t)) + 1e-12) * 0.953939
        ctx_768 = -0.000191848 + 0.999787 * (_ctx_768t + 0.3 * jax.random.normal(jax.random.fold_in(_rk, 611), (64, 77, 192), jnp.float32))
        return (x, ctx_768)
    x, ctx_768 = _rec_inputs()

    def _L0_xattn_setup():
        import jax, jax.numpy as jnp
        import numpy as np
        HEADS = 8
        DIM_HEAD = 64
        SCALE = DIM_HEAD ** (-0.5)
        key = jax.random.key(seed)
        ks = jax.random.split(key, 7)
        B, Nq, Nc = (4, 512, 512)
        Dq, Dc = (256, 192)
        inner = HEADS * DIM_HEAD
        x = jax.random.normal(ks[0], (B, Nq, Dq), dtype=jnp.float32)
        context = jax.random.normal(ks[1], (B, Nc, Dc), dtype=jnp.float32)
        Wq = jax.random.normal(ks[2], (Dq, inner), dtype=jnp.float32) * Dq ** (-0.5)
        Wk = jax.random.normal(ks[3], (Dc, inner), dtype=jnp.float32) * Dc ** (-0.5)
        Wv = jax.random.normal(ks[4], (Dc, inner), dtype=jnp.float32) * Dc ** (-0.5)
        Wo = jax.random.normal(ks[5], (inner, Dq), dtype=jnp.float32) * inner ** (-0.5)
        bo = jax.random.normal(ks[6], (Dq,), dtype=jnp.float32) * 0.01
        return {'x': x, 'context': context, 'Wq': Wq, 'Wk': Wk, 'Wv': Wv, 'Wo': Wo, 'bo': bo}
    _L0_xattn_all = _L0_xattn_setup()
    _L0_xattn_in = {k: v for k, v in _L0_xattn_all.items() if k in ('Wq', 'Wk', 'Wv', 'Wo', 'bo')}
    del _L0_xattn_all

    def _L0_ffn_setup():
        import jax, jax.numpy as jnp
        import numpy as np
        HIDDEN = 256
        HEAD_DIM = 64
        N_EXPERTS = 16
        MIN_EXPERTS = 2
        B, T = (4, 512)

        def _normalize(x, axis):
            n = jnp.sqrt(jnp.sum(x * x, axis=axis, keepdims=True))
            return x / jnp.maximum(n, 1e-12)

        def _ste(x):
            hard = jax.lax.stop_gradient((x > 0).astype(x.dtype))
            return hard + x - jax.lax.stop_gradient(x)

        def _gating(hidden_states, sim_matrix, gates):
            b, t, c = hidden_states.shape
            flat = hidden_states.reshape(b * t, c)
            logits = _normalize(flat, -1) @ _normalize(sim_matrix, 0) - jax.nn.sigmoid(gates)
            gated = jax.nn.relu(logits)
            mask = _ste(gated)
            inactive = jnp.sum(mask, axis=1) == 0
            _, fb_idx = jax.lax.top_k(logits, MIN_EXPERTS)
            fb = jnp.zeros_like(mask).at[jnp.arange(b * t)[:, None], fb_idx].set(1.0)
            fb_applied = inactive[:, None] & (fb > 0)
            mask = jnp.where(fb_applied, 1.0, mask)
            masked_logits = jnp.where(mask > 0, gated, -jnp.inf)
            return jax.nn.softmax(masked_logits, axis=-1).reshape(b, t, -1)
        key = jax.random.key(seed)
        ks = jax.random.split(key, 6)
        xav_qkv = float(np.sqrt(6.0 / (HIDDEN + HEAD_DIM)))
        return {'hidden_states': jax.random.normal(ks[0], (B, T, HIDDEN), dtype=jnp.float32), 'sim_matrix': jax.random.normal(ks[1], (HIDDEN, N_EXPERTS), dtype=jnp.float32), 'gates': jnp.zeros((N_EXPERTS,), dtype=jnp.float32), 'q_proj': jax.random.uniform(ks[2], (N_EXPERTS, HIDDEN, HEAD_DIM), jnp.float32, -xav_qkv, xav_qkv), 'k_proj': jax.random.uniform(ks[3], (N_EXPERTS, HIDDEN, HEAD_DIM), jnp.float32, -xav_qkv, xav_qkv), 'v_proj': jax.random.uniform(ks[4], (N_EXPERTS, HIDDEN, HEAD_DIM), jnp.float32, -xav_qkv, xav_qkv), 'o_proj': jax.random.uniform(ks[5], (N_EXPERTS, HEAD_DIM, HIDDEN), jnp.float32, -xav_qkv, xav_qkv)}
    _L0_ffn_all = _L0_ffn_setup()
    _L0_ffn_in = {k: v for k, v in _L0_ffn_all.items() if k in ('sim_matrix', 'gates', 'q_proj', 'k_proj', 'v_proj', 'o_proj')}
    del _L0_ffn_all
    return {'x': x, 'ctx_768': ctx_768, 'L0_xattn_Wq': _L0_xattn_in['Wq'], 'L0_xattn_Wk': _L0_xattn_in['Wk'], 'L0_xattn_Wv': _L0_xattn_in['Wv'], 'L0_xattn_Wo': _L0_xattn_in['Wo'], 'L0_xattn_bo': _L0_xattn_in['bo'], 'L0_ffn_sim_matrix': _L0_ffn_in['sim_matrix'], 'L0_ffn_gates': _L0_ffn_in['gates'], 'L0_ffn_q_proj': _L0_ffn_in['q_proj'], 'L0_ffn_k_proj': _L0_ffn_in['k_proj'], 'L0_ffn_v_proj': _L0_ffn_in['v_proj'], 'L0_ffn_o_proj': _L0_ffn_in['o_proj']}

def reference(x, ctx_768, L0_xattn_Wq, L0_xattn_Wk, L0_xattn_Wv, L0_xattn_Wo, L0_xattn_bo, L0_ffn_sim_matrix, L0_ffn_gates, L0_ffn_q_proj, L0_ffn_k_proj, L0_ffn_v_proj, L0_ffn_o_proj):
    import jax
    import jax.numpy as jnp

    def _L0_xattn_ref(x, context, Wq, Wk, Wv, Wo, bo):
        import jax, jax.numpy as jnp
        import numpy as np
        HEADS = 8
        DIM_HEAD = 64
        SCALE = DIM_HEAD ** (-0.5)
        B, Nq, _ = x.shape
        q = (x @ Wq).reshape(B, Nq, HEADS, DIM_HEAD)
        k = (context @ Wk).reshape(B, context.shape[1], HEADS, DIM_HEAD)
        v = (context @ Wv).reshape(B, context.shape[1], HEADS, DIM_HEAD)
        sim = jnp.einsum('bihd,bjhd->bhij', q, k) * SCALE
        attn = jax.nn.softmax(sim, axis=-1)
        out = jnp.einsum('bhij,bjhd->bihd', attn, v)
        out = out.reshape(B, Nq, HEADS * DIM_HEAD)
        return out @ Wo + bo

    def _L0_ffn_ref(hidden_states, sim_matrix, gates, q_proj, k_proj, v_proj, o_proj):
        import jax, jax.numpy as jnp
        import numpy as np
        HIDDEN = 256
        HEAD_DIM = 64
        N_EXPERTS = 16
        MIN_EXPERTS = 2
        B, T = (4, 512)

        def _normalize(x, axis):
            n = jnp.sqrt(jnp.sum(x * x, axis=axis, keepdims=True))
            return x / jnp.maximum(n, 1e-12)

        def _ste(x):
            hard = jax.lax.stop_gradient((x > 0).astype(x.dtype))
            return hard + x - jax.lax.stop_gradient(x)

        def _gating(hidden_states, sim_matrix, gates):
            b, t, c = hidden_states.shape
            flat = hidden_states.reshape(b * t, c)
            logits = _normalize(flat, -1) @ _normalize(sim_matrix, 0) - jax.nn.sigmoid(gates)
            gated = jax.nn.relu(logits)
            mask = _ste(gated)
            inactive = jnp.sum(mask, axis=1) == 0
            _, fb_idx = jax.lax.top_k(logits, MIN_EXPERTS)
            fb = jnp.zeros_like(mask).at[jnp.arange(b * t)[:, None], fb_idx].set(1.0)
            fb_applied = inactive[:, None] & (fb > 0)
            mask = jnp.where(fb_applied, 1.0, mask)
            masked_logits = jnp.where(mask > 0, gated, -jnp.inf)
            return jax.nn.softmax(masked_logits, axis=-1).reshape(b, t, -1)
        b, t, c = hidden_states.shape
        rw = _gating(hidden_states, sim_matrix, gates)
        q = jnp.einsum('bte,bted->btd', rw, jnp.einsum('btc,ecd->bted', hidden_states, q_proj))
        k = jnp.einsum('bte,bted->btd', rw, jnp.einsum('btc,ecd->bted', hidden_states, k_proj))
        v = jnp.einsum('bte,bted->btd', rw, jnp.einsum('btc,ecd->bted', hidden_states, v_proj))
        scale = 1.0 / jnp.sqrt(jnp.asarray(HEAD_DIM, dtype=q.dtype))
        scores = jnp.einsum('bqd,bkd->bqk', q, k) * scale
        causal = jnp.tril(jnp.ones((t, t), dtype=bool))
        scores = jnp.where(causal, scores, -jnp.inf)
        attn = jnp.einsum('bqk,bkd->bqd', jax.nn.softmax(scores, axis=-1), v)
        mixed = attn[:, :, None, :] * rw[..., None]
        return jnp.einsum('bted,edc->btc', mixed, o_proj)
    x = x + _L0_xattn_ref(_layernorm(x, axis=-1), ctx_768, L0_xattn_Wq, L0_xattn_Wk, L0_xattn_Wv, L0_xattn_Wo, L0_xattn_bo)
    x = x + _L0_ffn_ref(_layernorm(x, axis=-1), L0_ffn_sim_matrix, L0_ffn_gates, L0_ffn_q_proj, L0_ffn_k_proj, L0_ffn_v_proj, L0_ffn_o_proj)
    return x

_drawn_inputs = setup_inputs


def setup_inputs(seed=0):
    import zlib

    import numpy as np

    out = dict(_drawn_inputs(seed))
    spreads = {'L0_ffn_gates': (0.0, 0.1)}
    factors = {'L0_xattn_bo': 3.613}
    for name, (base, spread) in spreads.items():
        noise = np.random.default_rng([zlib.crc32(name.encode()), seed]).standard_normal(out[name].shape)
        drawn = base * np.exp(spread * noise) if base else spread * noise
        out[name] = jnp.asarray(drawn.astype(out[name].dtype))
    for name, factor in factors.items():
        out[name] = (out[name] * factor).astype(out[name].dtype)
    return out
```

```python
import concourse.bass as bass
from concourse import mybir
from concourse.alu_op_type import AluOpType as ALU
from contextlib import ExitStack

F32 = mybir.dt.float32
F32R = mybir.dt.float32r
U32 = mybir.dt.uint32
ACT = mybir.ActivationFunctionType
AX = mybir.AxisListType


def xattn_moe_kernel(nc, x, ctx_in, Wq, Wk, Wv, Wo, bo, sim_matrix, gates, q_proj, k_proj, v_proj, o_proj, out):
    B, T, C = x.shape
    NC, DC = ctx_in.shape[1:]
    P = 128
    NT = T // P
    CC = C // P
    INNER = Wq.shape[1]
    D = 64
    H = INNER // D
    HC = INNER // P
    NCE = NC + NC % 2
    DV = D + 2
    E = sim_matrix.shape[1]
    QKV = 3 * D
    EP = E // 2
    DK = DC // 2
    RG = 32
    EPS = 1e-5
    TINY = 1e-12
    SCALE = D ** -0.5
    MASKED = -1e30
    BIG = 3e38

    A_XT, A_CT, A_Q, A_K, A_V, A_S, A_AT, A_Y = 0, 1, 2, 4, 5, 6, 18, 20
    A_PT, A_PV = (10, 11, 14, 15), (12, 13, 16, 17)
    A_FILLS, A_BANKS = 21, 3
    B_XT, B_ROUTE, B_QKV = 0, 1, 2
    B_FILLS, B_BANKS = B_QKV + NT * EP, 3
    C_QK, C_S, C_PT, C_PV, C_AT, C_RW, C_Y = 0, 1, 2, 3, 4, 5, 9
    C_FILLS, C_BANKS = 10, 2
    assert A_FILLS % A_BANKS == 0 and B_FILLS % B_BANKS == 0 and C_FILLS % C_BANKS == 0
    HB = H // 2

    def a_at(n, fill):
        return A_FILLS * n + fill + 1

    def b_at(n, fill):
        return B_FILLS * n + fill + 1

    def c_at(n, fill):
        return C_FILLS * n + fill + 1

    def b_read(n, fill):
        return (B_QKV + 2 * NT * EP) * n + (fill + 1 if fill < B_QKV else 2 * fill)

    def c_read(n, fill):
        return (C_FILLS + 1) * n + fill + (1 if fill < C_S else 2)

    A_HI = {A_XT: 0, A_CT: 1, A_Q: 2, A_Q + 1: 3, A_K: 4, A_V: 5, A_PT[0]: 6, A_PT[1]: 7, A_PT[2]: 8,
            A_PT[3]: 9, A_AT: 10, A_AT + 1: 11}

    def a_hi_at(n, fill):
        return len(A_HI) * n + A_HI[fill] + 1

    def at(per_batch, n, which):
        return per_batch * n + which + 1

    def known(n):
        return isinstance(n, int)

    def on(n):
        return not known(n) or 0 <= n < B

    es = ExitStack()
    with es:
        def sb(name, shape, dt=F32):
            return es.enter_context(nc.sbuf_tensor(name, shape, dt))

        def split(name, shape):
            return sb(name + "_hi", shape, F32R), sb(name + "_lo", shape, F32R)

        def sem(name):
            return es.enter_context(nc.semaphore(name))

        wq = split("wq", [P, CC, INNER])
        wk = split("wk", [DK, 2, INNER])
        wv = split("wv", [DK, 2, INNER])
        wo = split("wo", [P, HC, C])
        wqkv = split("wqkv", [P, CC, E, QKV])
        wo2 = split("wo2", [P, EP, C])
        wsim = split("wsim", [P, CC, E])
        bo_all = sb("bo_all", [P, C])
        sig = sb("sig", [P, E])
        ident = sb("ident", [P, P])
        causal = sb("causal", [P, T])
        expo = sb("expo", [P, 2 * NT])
        iota_i = sb("iota_i", [P, E], mybir.dt.int32)
        iota = sb("iota", [P, E])
        sim_n = sb("sim_n", [P, E])
        half_e = sb("half_e", [P, E])
        xt = sb("xt", [P, NT, C])
        xb = sb("xb", [P, NT, C])
        xn = sb("xn", [P, NT, C])
        x2a = sb("x2a", [P, NT, C])
        x2b = sb("x2b", [P, NT, C])
        x2n = sb("x2n", [P, NT, C])
        stats = [sb(f"stats{k}", [P, NT, 6]) for k in (1, 2)]
        mv = [sb(f"mv{k}", [P, NT, 2]) for k in (1, 2)]
        pow_in = [sb(f"pow_in{k}", [P, 2, NT]) for k in (1, 2)]
        pow_out = [sb(f"pow_out{k}", [P, 2, NT]) for k in (1, 2)]
        rn = sb("rn", [P, 3, NT])
        ct = sb("ct", [NC, DC])
        xT = split("xT", [P, CC, T])
        cT = split("cT", [DK, 2, NCE])
        qT = split("qT", [P, HC, T])
        kT = split("kT", [P, HC, NCE])
        v = split("v", [NC, H, DV])
        s_max = sb("s_max", [P, 2 * NT, HB])
        probs = sb("probs", [P, NT, H, NC])
        pT = split("pT", [NC, H, P])
        r_sum = sb("r_sum", [P, 2 * NT, HB])
        attn = sb("attn", [P, NT, HC, 2, D])
        aT = split("aT", [P, NT, HC, P])
        x2T = split("x2T", [P, CC, T])
        rwT = sb("rwT", [2 * RG, T], F32R)
        sel = sb("sel", [2 * RG, EP, P], F32R)
        z = sb("z", [P, NT, E])
        top = sb("top", [P, NT, 8])
        idx = sb("idx", [P, NT, 8], U32)
        idxf = sb("idxf", [P, NT, 8])
        z_top = sb("z_top", [P, NT])
        idle = sb("idle", [P, NT])
        first = sb("first", [P, NT, E])
        second = sb("second", [P, NT, E])
        act_on = sb("act_on", [P, NT, E])
        g = sb("g", [P, NT, E])
        w = sb("w", [P, NT, E])
        w_sum = sb("w_sum", [P, 2, NT])
        rw = sb("rw", [P, NT, E])
        rw_c = sb("rw_c", [P, NT, 2 * RG])
        acc = sb("acc", [P, NT, 2, QKV])
        qkv = sb("qkv", [P, NT, QKV])
        qkT = split("qkT", [D, 2, T])
        v2 = split("v2", [P, NT, D])
        m2 = sb("m2", [P, NT])
        p2 = sb("p2", [P, P + T])
        p2_sum = sb("p2_sum", [P, 2, NT])
        p2T = split("p2T", [P, 3, P])
        attn2 = sb("attn2", [P, NT, 2, D])
        aT2 = sb("aT2", [P, T])
        mix = sb("mix", [P, EP, T])
        mixs = split("mixs", [P, EP, T])
        y = mix[:, EP - NT:EP, :]

        banks_a = [es.enter_context(nc.psum_tensor(f"bank_a{k}", [P, 512], F32)) for k in range(A_BANKS)]
        banks_b = [es.enter_context(nc.psum_tensor(f"bank_b{k}", [P, 512], F32)) for k in range(B_BANKS)]
        banks_c = [es.enter_context(nc.psum_tensor(f"bank_c{k}", [P, 512], F32)) for k in range(C_BANKS)]

        def bank_a(fill):
            return banks_a[fill % A_BANKS]

        def bank_b(fill):
            return banks_b[fill % B_BANKS]

        def bank_c(fill):
            return banks_c[fill % C_BANKS]

        a_fill, a_hi, a_evac = sem("a_fill"), sem("a_hi"), sem("a_evac")
        b_fill, b_hi, b_evac = sem("b_fill"), sem("b_hi"), sem("b_evac")
        c_fill, c_hi, c_evac = sem("c_fill"), sem("c_hi"), sem("c_evac")
        x_in, ct_in, y_out = sem("x_in"), sem("ct_in"), sem("y_out")
        ln_stats = [sem(f"ln_stats{k}") for k in (1, 2)]
        ln_var = [sem(f"ln_var{k}") for k in (1, 2)]
        ln_pow = [sem(f"ln_pow{k}") for k in (1, 2)]
        ln_done = [sem(f"ln_done{k}") for k in (1, 2)]
        rn_step = sem("rn_step")
        xb_ready, x2_moved = sem("xb_ready"), sem("x2_moved")
        s_max_ready, p_ready, r_sum_ready = sem("s_max_ready"), sem("p_ready"), sem("r_sum_ready")
        top_ready, idx_ready = sem("top_ready"), sem("idx_ready")
        pool_step = sem("pool_step")
        g_ready, e_ready, w_ready, w_sum_ready = sem("g_ready"), sem("e_ready"), sem("w_ready"), sem("w_sum_ready")
        rw_ready, rw_c_ready, qkv_ready, v2_ready = sem("rw_ready"), sem("rw_c_ready"), sem("qkv_ready"), sem("v2_ready")
        p2_ready, r2_ready, aT2_ready = sem("p2_ready"), sem("r2_ready"), sem("aT2_ready")
        mix_hi, mix_lo = sem("mix_hi"), sem("mix_lo")
        consts, wt_in, wt_hi, wt_ready = sem("consts"), [sem("wt_in0"), sem("wt_in1")], sem("wt_hi"), sem("wt_ready")
        small_in, sig_step, sim_step, sim_norm = sem("small_in"), sem("sig_step"), sem("sim_step"), sem("sim_norm")
        pad_done = sem("pad_done")
        passed = sem("passed")

        setup = acc[:, :, :, :].rearrange("p a b c -> p (a b c)")
        ones = setup[:, 0:P]
        sim_raw, sim_sq = [setup[:, P + k * CC * E:P + (k + 1) * CC * E].rearrange("p (a b) -> p a b", a=CC) for k in range(2)]
        sel_raw = probs[:, :, :, :].rearrange("p a b c -> p (a b c)")[0:2 * RG, 0:EP * P]
        def apart(eng):
            eng.sem_inc(passed, 1)

        SP_COLS = EP * T // 2
        stage = [mix[:, k * EP // 2:(k + 1) * EP // 2, :].rearrange("p a b -> p (a b)") for k in range(2)]
        E4 = E // 4

        def proj_piece(cc, quarter):
            e0, e1 = quarter * E4, (quarter + 1) * E4
            loads = [(lambda s, k=k: s[:, 0:E4 * QKV].rearrange("p (e f) -> p e f", f=QKV)[:, :, k * D:(k + 1) * D],
                      w_[e0:e1, cc * P:(cc + 1) * P, :].rearrange("e c d -> c e d"))
                     for k, w_ in enumerate((q_proj, k_proj, v_proj))]
            return loads, E4 * QKV, P, [t[:, cc, e0:e1, :].rearrange("p e f -> p (e f)") for t in wqkv]

        def chunked_piece(dst, src, n):
            rows, cols = src.shape[0], src.shape[2]
            return ([(lambda s: s[0:rows, 0:n * cols].rearrange("p (a b) -> p a b", a=n), src)], n * cols, rows,
                    [t.rearrange("p a b -> p (a b)") for t in dst])

        wo2_rows = o_proj.rearrange("(a e) d b -> (e d) a b", e=2)
        PIECES = [
            chunked_piece([t[:, :, :] for t in wq], Wq.rearrange("(a p) b -> p a b", p=P), CC),
            chunked_piece([t[:, :, :] for t in wk], Wk.rearrange("(a p) b -> p a b", p=DK), 2),
            chunked_piece([t[:, :, :] for t in wv], Wv.rearrange("(a p) b -> p a b", p=DK), 2),
            chunked_piece([t[:, :, :] for t in wo], Wo.rearrange("(a p) b -> p a b", p=P), HC),
            *[proj_piece(cc, quarter) for quarter in range(4) for cc in range(CC)],
            *[chunked_piece([t[:, k * EP // 2:(k + 1) * EP // 2, :] for t in wo2],
                            wo2_rows[:, k * EP // 2:(k + 1) * EP // 2, :], EP // 2) for k in range(2)],
        ]
        W_Q, W_K, W_V, W_O, W_QKV, W_O2 = 0, 1, 2, 3, 11, 13
        assert len(PIECES) == W_O2 + 1 and all(cols <= SP_COLS for _, cols, _, _ in PIECES)

        def loads_before(piece, slot):
            return sum(len(PIECES[k][0]) for k in range(slot, piece + 1, 2))

        block = es.enter_context(nc.Block())

        @block.sync
        def _(sp):
            def load_x(n):
                if not (known(n) and n == 0):
                    sp.wait_ge(xb_ready, at(1, n - 1, 0))
                    sp.wait_ge(ln_done[0], at(NT, n - 1, NT - 1))
                sp.dma_start(xt[:, :, :], x[n, :, :].rearrange("(t p) c -> p t c", p=P)).then_inc(x_in, 16)

            def load_ctx(n):
                if not (known(n) and n == 0):
                    sp.wait_ge(a_fill, a_at(n - 1, A_CT))
                sp.dma_start(ct[:, :], ctx_in[n, :, :]).then_inc(ct_in, 16)

            def store(n):
                sp.wait_ge(c_evac, c_read(n, C_Y))
                sp.dma_start(out[n, :, :].rearrange("(t p) c -> p t c", p=P), y[:, :, :]).then_inc(y_out, 16)

            load_x(0)
            load_ctx(0)
            sp.dma_start(sim_raw[:, :, :], sim_matrix.rearrange("(a p) e -> p a e", p=P)).then_inc(small_in, 16)
            sp.dma_start(sig[:, :], gates.partition_broadcast(P)).then_inc(small_in, 16)
            sp.dma_start(bo_all[:, :], bo.partition_broadcast(P)).then_inc(small_in, 16)
            for k, (loads, cols, rows, dst) in enumerate(PIECES):
                if k >= 2:
                    sp.wait_ge(wt_ready, k - 1)
                for view, src in loads:
                    sp.dma_start(view(stage[k % 2]), src).then_inc(wt_in[k % 2], 16)

            def step(i):
                if on(i + 2):
                    load_ctx(i + 2)
                if on(i - 2):
                    store(i - 2)
                if on(i + 2):
                    load_x(i + 2)

            for i in range(-1, 3):
                step(i)
            with sp.Fori(3, B - 2) as i:
                step(i)
            for i in range(B - 2, B + 2):
                step(i)
            sp.wait_ge(y_out, 16 * B)

        @block.tensor
        def _(pe):
            def product(dst, lhs, rhs, start=True, stop=True):
                nc.tensor.matmul(dst, lhs[1], rhs[0], start=start, stop=False)
                nc.tensor.matmul(dst, lhs[0], rhs[1], start=False, stop=False)
                return nc.tensor.matmul(dst, lhs[0], rhs[0], start=False, stop=stop)

            def part(pair, *at_):
                return [t[at_] for t in pair]

            def ring_a(n, fill):
                if not (known(n) and n == 0 and fill < A_BANKS):
                    pe.wait_ge(a_evac, a_at(n, fill - A_BANKS))

            def ring_b(n, fill):
                if not (known(n) and n == 0 and fill < B_BANKS):
                    if fill >= B_BANKS:
                        pe.wait_ge(b_evac, b_read(n, fill - B_BANKS))
                    else:
                        pe.wait_ge(b_evac, b_read(n - 1, fill - B_BANKS + B_FILLS))

            def ring_c(n, fill):
                if not (known(n) and n == 0 and fill < C_BANKS):
                    if fill >= C_BANKS:
                        pe.wait_ge(c_evac, c_read(n, fill - C_BANKS))
                    else:
                        pe.wait_ge(c_evac, c_read(n - 1, fill - C_BANKS + C_FILLS))

            def weights(n, piece):
                if known(n) and n == 0:
                    pe.wait_ge(wt_ready, piece + 1)

            def a_xT(n):
                ring_a(n, A_XT)
                pe.wait_ge(ln_done[0], at(NT, n, NT - 1))
                for cc in range(CC):
                    for t in range(NT):
                        last = nc.tensor.transpose(bank_a(A_XT)[:, cc * T + t * P:cc * T + (t + 1) * P],
                                                   xn[:, t, cc * P:(cc + 1) * P], ident[:, :])
                last.then_inc(a_fill, 1)

            def a_cT(n):
                ring_a(n, A_CT)
                pe.wait_ge(ct_in, 16 * (n + 1))
                for k in range(2):
                    last = nc.tensor.transpose(bank_a(A_CT)[0:DK, k * P:k * P + NC], ct[:, k * DK:(k + 1) * DK],
                                               ident[0:NC, 0:NC])
                last.then_inc(a_fill, 1)

            def a_q(n, j):
                fill = A_Q + j
                ring_a(n, fill)
                weights(n, W_Q)
                pe.wait_ge(a_evac, a_at(n, A_XT))
                for k in range(2):
                    hc = 2 * j + k
                    for cc in range(CC):
                        last = product(bank_a(fill)[:, k * T:(k + 1) * T],
                                       part(wq, slice(None), cc, slice(hc * P, (hc + 1) * P)),
                                       part(xT, slice(None), cc, slice(None)), cc == 0, cc == CC - 1)
                last.then_inc(a_fill, 1)

            def a_k(n):
                ring_a(n, A_K)
                weights(n, W_K)
                pe.wait_ge(a_evac, a_at(n, A_CT))
                for hc in range(HC):
                    dst = bank_a(A_K)[:, hc * NCE:(hc + 1) * NCE]
                    hs = slice(hc * P, (hc + 1) * P)
                    for k in range(2):
                        last = product(dst, part(wk, slice(None), k, hs), part(cT, slice(None), k, slice(None)), k == 0, k == 1)
                last.then_inc(a_fill, 1)

            def a_v(n):
                ring_a(n, A_V)
                weights(n, W_V)
                dst = bank_a(A_V)[0:NC, :]
                for k in range(2):
                    last = product(dst, part(cT, slice(None), k, slice(0, NC)), part(wv, slice(None), k, slice(None)),
                                   k == 0, k == 1)
                last.then_inc(a_fill, 1)

            def a_s(n, j):
                fill, t = A_S + j, j // 2
                ring_a(n, fill)
                pe.wait_ge(a_evac, a_at(n, A_K))
                for k in range(HB):
                    h = 2 * k + j % 2
                    rows = slice((h % 2) * D, (h % 2 + 1) * D)
                    last = product(bank_a(fill)[:, k * NCE:(k + 1) * NCE],
                                   part(qT, rows, h // 2, slice(t * P, (t + 1) * P)), part(kT, rows, h // 2, slice(None)))
                last.then_inc(a_fill, 1)

            def a_pT(n, j):
                fill, t = A_PT[j], j // 2
                ring_a(n, fill)
                pe.wait_ge(p_ready, at(2 * NT, n, j))
                for k in range(HB):
                    last = nc.tensor.transpose(bank_a(fill)[0:NC, k * P:(k + 1) * P],
                                               probs[:, t, (j % 2) * HB + k, :], ident[:, :])
                last.then_inc(a_fill, 1)

            def a_pv(n, j):
                fill, t = A_PV[j], j // 2
                ring_a(n, fill)
                if known(n) and n == 0:
                    pe.wait_ge(pad_done, 3)
                pe.wait_ge(a_evac, a_at(n, A_PT[j]))
                for k in range(HB):
                    h = 2 * k + j % 2
                    last = product(bank_a(fill)[:, k * DV:(k + 1) * DV],
                                   part(pT, slice(None), (j % 2) * HB + k, slice(None)), part(v, slice(None), h, slice(None)))
                last.then_inc(a_fill, 1)

            def a_aT(n, t):
                fill = A_AT + t
                ring_a(n, fill)
                pe.wait_ge(a_evac, a_at(n, A_PV[2 * t + 1]))
                for hc in range(HC):
                    last = nc.tensor.transpose(bank_a(fill)[:, hc * P:(hc + 1) * P],
                                               attn[:, t, hc, :, :].rearrange("p a b -> p (a b)"), ident[:, :])
                last.then_inc(a_fill, 1)

            def a_y(n):
                ring_a(n, A_Y)
                weights(n, W_O)
                pe.wait_ge(a_evac, a_at(n, A_AT + 1))
                for t in range(NT):
                    for hc in range(HC):
                        last = product(bank_a(A_Y)[:, t * C:(t + 1) * C], part(aT, slice(None), t, hc, slice(None)),
                                       part(wo, slice(None), hc, slice(None)), hc == 0, hc == HC - 1)
                last.then_inc(a_fill, 1)

            def b_xT(n):
                ring_b(n, B_XT)
                pe.wait_ge(ln_done[1], at(NT, n, NT - 1))
                for cc in range(CC):
                    for t in range(NT):
                        last = nc.tensor.transpose(bank_b(B_XT)[:, cc * T + t * P:cc * T + (t + 1) * P],
                                                   x2n[:, t, cc * P:(cc + 1) * P], ident[:, :])
                last.then_inc(b_fill, 1)

            def b_route(n):
                ring_b(n, B_ROUTE)
                if known(n) and n == 0:
                    pe.wait_ge(sim_step, 6)
                pe.wait_ge(b_evac, b_read(n, B_XT))
                for t in range(NT):
                    for cc in range(CC):
                        last = product(bank_b(B_ROUTE)[:, t * E:(t + 1) * E],
                                       part(x2T, slice(None), cc, slice(t * P, (t + 1) * P)),
                                       part(wsim, slice(None), cc, slice(None)), cc == 0, cc == CC - 1)
                last.then_inc(b_fill, 1)

            def b_qkv(n, j):
                fill, t, ep = B_QKV + j, j // EP, j % EP
                ring_b(n, fill)
                weights(n, W_QKV)
                for cc in range(CC):
                    last = product(bank_b(fill)[:, 0:2 * QKV], part(x2T, slice(None), cc, slice(t * P, (t + 1) * P)),
                                   [w_[:, cc, 2 * ep:2 * ep + 2, :].rearrange("p a b -> p (a b)") for w_ in wqkv],
                                   cc == 0, cc == CC - 1)
                last.then_inc(b_fill, 1)

            def c_qk(n):
                ring_c(n, C_QK)
                pe.wait_ge(qkv_ready, at(NT, n, NT - 1))
                apart(pe)
                for k in range(2):
                    for t in range(NT):
                        last = nc.tensor.transpose(bank_c(C_QK)[0:D, k * T + t * P:k * T + (t + 1) * P],
                                                   qkv[:, t, k * D:(k + 1) * D], ident[:, :])
                last.then_inc(c_fill, 1)

            def c_s(n):
                ring_c(n, C_S)
                pe.wait_ge(c_evac, c_read(n, C_QK))
                for t in range(NT):
                    keys = (t + 1) * P
                    last = product(bank_c(C_S)[:, t * P:t * P + keys], part(qkT, slice(None), 0, slice(t * P, (t + 1) * P)),
                                   part(qkT, slice(None), 1, slice(0, keys)))
                last.then_inc(c_fill, 1)

            def c_pT(n):
                ring_c(n, C_PT)
                pe.wait_ge(p2_ready, at(NT, n, NT - 1))
                for k in range(3):
                    last = nc.tensor.transpose(bank_c(C_PT)[:, k * P:(k + 1) * P], p2[:, k * P:(k + 1) * P], ident[:, :])
                last.then_inc(c_fill, 1)

            def c_pv(n):
                ring_c(n, C_PV)
                pe.wait_ge(c_evac, c_read(n, C_PT))
                pe.wait_ge(v2_ready, at(2, n, 1))
                product(bank_c(C_PV)[:, 0:D], part(p2T, slice(None), 0, slice(None)), part(v2, slice(None), 0, slice(None)))
                product(bank_c(C_PV)[:, D:2 * D], part(p2T, slice(None), 1, slice(None)),
                        part(v2, slice(None), 0, slice(None)), True, False)
                product(bank_c(C_PV)[:, D:2 * D], part(p2T, slice(None), 2, slice(None)),
                        part(v2, slice(None), 1, slice(None)), False, True).then_inc(c_fill, 1)

            def c_aT(n):
                ring_c(n, C_AT)
                pe.wait_ge(rw_c_ready, at(2, n, 1))
                apart(pe)
                for t in range(NT):
                    nc.tensor.transpose(bank_c(C_AT)[0:2 * RG, T + t * P:T + (t + 1) * P], rw_c[:, t, :], ident[:, :])
                pe.wait_ge(c_evac, c_read(n, C_PV))
                for t in range(NT):
                    last = nc.tensor.transpose(bank_c(C_AT)[:, t * P:(t + 1) * P],
                                               attn2[:, t, :, :].rearrange("p a b -> p (a b)"), ident[:, :])
                last.then_inc(c_fill, 1)

            def c_rw(n, j):
                fill = C_RW + j
                ring_c(n, fill)
                pe.wait_ge(c_evac, c_read(n, C_AT))
                for k in range(2):
                    last = nc.tensor.matmul(bank_c(fill)[:, k * T:(k + 1) * T], sel[:, 2 * j + k, :], rwT[:, :],
                                            start=True, stop=True)
                last.then_inc(c_fill, 1)

            def c_y(n):
                ring_c(n, C_Y)
                weights(n, W_O2)
                for t in range(NT):
                    for ep in range(EP):
                        if t == 0 and ep % 2 == 0:
                            pe.wait_ge(mix_lo, at(4, n, ep // 2))
                        last = product(bank_c(C_Y)[:, t * C:(t + 1) * C],
                                       part(mixs, slice(None), ep, slice(t * P, (t + 1) * P)),
                                       part(wo2, slice(None), ep, slice(None)), ep == 0, ep == EP - 1)
                last.then_inc(c_fill, 1)

            def sim_norms():
                pe.wait_ge(consts, 4)
                pe.wait_ge(sim_step, 1)
                for cc in range(CC):
                    last = nc.tensor.matmul(bank_b(B_ROUTE)[:, 0:E], ones[:, :], sim_sq[:, cc, :], start=cc == 0, stop=cc == CC - 1)
                last.then_inc(sim_norm, 1)

            sim_norms()

            def step(i):
                h, a, b, c = i + 1, i, i - 1, i - 2

                def do_a(fn, *k):
                    if on(a):
                        fn(a, *k)

                def do_b(*js):
                    for j in js:
                        if on(b):
                            b_qkv(b, j)

                def do_c(fn, *k):
                    if on(c):
                        fn(c, *k)

                do_c(c_qk)
                do_a(a_q, 0)
                do_c(c_s)
                if on(b):
                    b_route(b)
                do_a(a_q, 1)
                do_a(a_k)
                do_c(c_pT)
                do_a(a_v)
                do_c(c_pv)
                do_a(a_s, 0)
                do_a(a_s, 1)
                do_c(c_aT)
                do_b(0)
                do_c(c_rw, 0)
                do_a(a_s, 2)
                do_b(1)
                do_c(c_rw, 1)
                do_a(a_s, 3)
                do_b(2)
                do_c(c_rw, 2)
                do_a(a_pT, 0)
                do_b(3)
                do_c(c_rw, 3)
                do_a(a_pT, 1)
                do_b(4)
                do_b(5)
                do_a(a_pv, 0)
                do_a(a_pv, 1)
                do_a(a_pT, 2)
                do_b(6)
                do_a(a_pT, 3)
                do_b(7)
                do_c(c_y)
                do_a(a_pv, 2)
                do_a(a_pv, 3)
                do_b(8)
                do_a(a_aT, 0)
                do_b(9)
                do_a(a_aT, 1)
                do_b(10, 11)
                do_a(a_y)
                do_b(12)
                if on(h):
                    a_xT(h)
                do_b(13)
                if on(h):
                    a_cT(h)
                do_b(14, 15)
                if on(a):
                    b_xT(a)

            for i in range(-1, 3):
                step(i)
            with pe.Fori(3, B - 2) as i:
                step(i)
            for i in range(B - 2, B + 2):
                step(i)

        @block.scalar
        def _(act):
            copy = ACT.Copy

            act.wait_ge(small_in, 48)
            nc.scalar.activation(half_e[:, :], sig[:, :], ACT.Exp, scale=-1.0).then_inc(sig_step, 1)
            for k, (loads, cols, rows, dst) in enumerate(PIECES):
                act.wait_ge(wt_in[k % 2], 16 * loads_before(k, k % 2))
                nc.scalar.activation(dst[0], stage[k % 2][0:rows, 0:cols], copy).then_inc(wt_hi, 1)

            def a_part(n, fill, dst, src):
                act.wait_ge(a_fill, a_at(n, fill))
                nc.scalar.activation(dst, src, copy).then_inc(a_hi, 1)

            def a_xT(n):
                a_part(n, A_XT, xT[0][:, :, :].rearrange("p a b -> p (a b)"), bank_a(A_XT)[:, :])

            def a_cT(n):
                if known(n) and n == 0:
                    act.wait_ge(pad_done, 2)
                src = bank_a(A_CT)[0:DK, 0:2 * P].rearrange("p (a b) -> p a b", a=2)
                a_part(n, A_CT, cT[0][:, :, 0:NC], src[:, :, 0:NC])

            def a_q(n, j):
                a_part(n, A_Q + j, qT[0][:, 2 * j:2 * j + 2, :].rearrange("p a b -> p (a b)"), bank_a(A_Q + j)[:, :])

            def a_k(n):
                a_part(n, A_K, kT[0][:, :, :].rearrange("p a b -> p (a b)"), bank_a(A_K)[:, 0:HC * NCE])

            def a_v(n):
                if known(n) and n == 0:
                    act.wait_ge(pad_done, 3)
                a_part(n, A_V, v[0][:, :, 0:D], bank_a(A_V)[0:NC, :].rearrange("p (a b) -> p a b", a=H))

            def a_exp(n, j):
                act.wait_ge(a_evac, a_at(n, A_S + j))
                hs = slice((j % 2) * HB, (j % 2 + 1) * HB)
                nc.scalar.activation(probs[:, j // 2, hs, :], probs[:, j // 2, hs, :], ACT.Exp,
                                     scale=SCALE).then_inc(p_ready, 1)

            def a_pT(n, j):
                a_part(n, A_PT[j], pT[0][:, (j % 2) * HB:(j % 2 + 1) * HB, :].rearrange("p a b -> p (a b)"), bank_a(A_PT[j])[0:NC, :])

            def a_aT(n, t):
                a_part(n, A_AT + t, aT[0][:, t, :, :].rearrange("p a b -> p (a b)"), bank_a(A_AT + t)[:, :])

            def b_xT(n):
                act.wait_ge(b_fill, b_at(n, B_XT))
                nc.scalar.activation(x2T[0][:, :, :].rearrange("p a b -> p (a b)"), bank_b(B_XT)[:, :], copy).then_inc(b_hi, 1)

            def b_exp(n):
                act.wait_ge(g_ready, at(1, n, 0))
                nc.scalar.activation(w[:, :, :], g[:, :, :], ACT.Exp).then_inc(e_ready, 1)

            def c_part(n, fill, dst, src):
                act.wait_ge(c_fill, c_at(n, fill))
                nc.scalar.activation(dst, src, copy).then_inc(c_hi, 1)

            def c_qk(n):
                c_part(n, C_QK, qkT[0][:, :, :].rearrange("p a b -> p (a b)"), bank_c(C_QK)[0:D, :])

            def c_exp(n):
                for t in range(NT):
                    keys = slice(t * P, t * P + (t + 1) * P)
                    act.wait_ge(c_evac, c_read(n, C_S) - NT + 1 + t)
                    nc.scalar.activation(p2[:, keys], p2[:, keys], ACT.Exp, bias=m2[:, t:t + 1], scale=-1.0,
                                         accum_out=p2_sum[:, 0, t:t + 1]).then_inc(p2_ready, 1)

            def c_pT(n):
                c_part(n, C_PT, p2T[0][:, :, :].rearrange("p a b -> p (a b)"), bank_c(C_PT)[:, 0:3 * P])

            def c_aT(n):
                act.wait_ge(c_fill, c_at(n, C_AT))
                nc.scalar.activation(aT2[:, :], bank_c(C_AT)[:, 0:T], copy).then_inc(aT2_ready, 1)
                nc.scalar.activation(rwT[:, :], bank_c(C_AT)[0:2 * RG, T:2 * T], copy).then_inc(c_hi, 1)

            def c_mix(n, j):
                act.wait_ge(c_evac, c_read(n, C_RW + j))
                nc.scalar.activation(mixs[0][:, 2 * j:2 * j + 2, :], mix[:, 2 * j:2 * j + 2, :], copy).then_inc(mix_hi, 1)

            def step(i):
                h, a, b, c = i + 1, i, i - 1, i - 2

                def do(n, fn, *k):
                    if on(n):
                        fn(n, *k)

                do(c, c_qk)
                do(a, a_q, 0)
                do(c, c_exp)
                do(a, a_q, 1)
                do(b, b_exp)
                do(a, a_k)
                do(c, c_pT)
                do(a, a_v)
                do(a, a_exp, 0)
                do(a, a_exp, 1)
                do(c, c_aT)
                do(c, c_mix, 0)
                do(a, a_exp, 2)
                do(c, c_mix, 1)
                do(a, a_exp, 3)
                do(a, a_pT, 0)
                do(c, c_mix, 2)
                do(a, a_pT, 1)
                do(c, c_mix, 3)
                do(a, a_pT, 2)
                do(a, a_pT, 3)
                do(a, a_aT, 0)
                do(a, a_aT, 1)
                do(h, a_xT)
                do(h, a_cT)
                do(a, b_xT)

            for i in range(-1, 3):
                step(i)
            with act.Fori(3, B - 2) as i:
                step(i)
            for i in range(B - 2, B + 2):
                step(i)

        @block.vector
        def _(dve):
            V = nc.vector

            V.memset(expo[:, 0:NT], -0.5).then_inc(consts, 1)
            V.memset(expo[:, NT:2 * NT], 0.5).then_inc(consts, 1)
            V.memset(ones[:, :], 1.0).then_inc(consts, 1)
            for k in range(2):
                V.memset(cT[k].bitcast(F32)[:, :, NC:NCE], 0.0)
                V.memset(v[k].bitcast(F32)[:, :, D:DV], 0.0).then_inc(pad_done, 1)
            dve.wait_ge(pad_done, 2)
            V.memset(v[0].bitcast(F32)[:, :, D:D + 1], 1.0).then_inc(pad_done, 1)
            dve.wait_ge(small_in, 48)
            V.tensor_tensor(sim_sq[:, :, :], sim_raw[:, :, :], sim_raw[:, :, :], ALU.mult).then_inc(sim_step, 1)
            dve.wait_ge(sim_norm, 1)
            V.tensor_copy(sim_n[:, :], bank_b(B_ROUTE)[:, 0:E]).then_inc(sim_norm, 1)
            dve.wait_ge(sim_norm, 3)
            V.tensor_scalar(sim_n[:, :], sim_n[:, :], TINY, None, ALU.max).then_inc(sim_norm, 1)
            dve.wait_ge(sim_norm, 4)
            V.reciprocal(sim_n[:, :], sim_n[:, :]).then_inc(sim_step, 1)
            dve.wait_ge(sim_step, 2)
            V.tensor_tensor(sim_sq[:, :, :], sim_raw[:, :, :], sim_n[:, :].unsqueeze(1).to_broadcast([P, CC, E]),
                            ALU.mult).then_inc(sim_step, 1)
            dve.wait_ge(sim_step, 3)
            V.tensor_copy(wsim[0][:, :, :], sim_sq[:, :, :]).then_inc(sim_step, 1)
            dve.wait_ge(sim_step, 4)
            V.tensor_tensor(wsim[1][:, :, :], sim_sq[:, :, :], wsim[0].bitcast(F32)[:, :, :], ALU.subtract).then_inc(sim_step, 1)
            dve.wait_ge(sig_step, 1)
            V.tensor_scalar(half_e[:, :], half_e[:, :], 1.0, None, ALU.add).then_inc(sig_step, 1)
            dve.wait_ge(sig_step, 2)
            V.reciprocal(sig[:, :], half_e[:, :]).then_inc(sig_step, 1)
            dve.wait_ge(pool_step, 8)
            V.tensor_copy(sel[:, :, :].rearrange("p a b -> p (a b)"), sel_raw).then_inc(sim_step, 1)
            for k, (loads, cols, rows, dst) in enumerate(PIECES):
                dve.wait_ge(wt_hi, k + 1)
                V.tensor_tensor(dst[1], stage[k % 2][0:rows, 0:cols], dst[0].bitcast(F32), ALU.subtract).then_inc(wt_ready, 1)

            def ln_a(k, n, src):
                for t in range(NT):
                    V.bn_stats(stats[k][:, t, :], src[:, t, :]).then_inc(ln_stats[k], 1)
                for t in range(NT):
                    dve.wait_ge(ln_stats[k], at(2 * NT, n, t))
                    apart(dve)
                    V.bn_aggr(mv[k][:, t, :], stats[k][:, t, :]).then_inc(ln_stats[k], 1)
                dve.wait_ge(ln_stats[k], at(2 * NT, n, 2 * NT - 1))
                if k == 0:
                    V.tensor_scalar(pow_in[k][:, 0, :], mv[k][:, :, 1], EPS, None, ALU.add).then_inc(ln_var[k], 1)
                else:
                    V.tensor_scalar(pow_in[k][:, 0, :], mv[k][:, :, 1], EPS, None, ALU.add).then_inc(ln_var[k], 1)
                    V.tensor_scalar(pow_in[k][:, 1, :], mv[k][:, :, 1], float(C), None, ALU.mult).then_inc(ln_var[k], 1)

            def ln_b(k, n, src, dst):
                dve.wait_ge(ln_pow[k], at(1, n, 0))
                for t in range(NT):
                    V.tensor_scalar(dst[:, t, :], src[:, t, :], mv[k][:, t, 0:1], pow_out[k][:, 0, t:t + 1],
                                    ALU.subtract, ALU.mult).then_inc(ln_done[k], 1)

            def ln1_a(n):
                dve.wait_ge(x_in, 16 * (n + 1))
                ln_a(0, n, xt)

            def ln1_b(n):
                if not (known(n) and n == 0):
                    dve.wait_ge(a_fill, a_at(n - 1, A_XT))
                ln_b(0, n, xt, xn)

            def ln2_a(n):
                dve.wait_ge(a_evac, a_at(n, A_Y))
                ln_a(1, n, x2a)

            def ln2_b(n):
                if not (known(n) and n == 0):
                    dve.wait_ge(b_fill, b_at(n - 1, B_XT))
                ln_b(1, n, x2a, x2n)
                V.tensor_tensor(rn[:, 0, :], pow_out[1][:, 0, :], pow_out[1][:, 1, :], ALU.mult).then_inc(rn_step, 1)
                dve.wait_ge(rn_step, at(3, n, 0))
                V.tensor_scalar(rn[:, 1, :], rn[:, 0, :], TINY, None, ALU.max).then_inc(rn_step, 1)
                dve.wait_ge(rn_step, at(3, n, 1))
                V.reciprocal(rn[:, 2, :], rn[:, 1, :]).then_inc(rn_step, 1)

            def a_part(n, fill, pair, src):
                dve.wait_ge(a_hi, a_hi_at(n, fill))
                V.tensor_tensor(pair[1], src, pair[0].bitcast(F32), ALU.subtract).then_inc(a_evac, 1)

            def flat(pair, *at_):
                return [t[at_].rearrange("p a b -> p (a b)") for t in pair]

            def a_xT(n):
                a_part(n, A_XT, flat(xT, slice(None), slice(None), slice(None)), bank_a(A_XT)[:, :])

            def a_cT(n):
                src = bank_a(A_CT)[0:DK, 0:2 * P].rearrange("p (a b) -> p a b", a=2)
                a_part(n, A_CT, [t[:, :, 0:NC] for t in cT], src[:, :, 0:NC])

            def a_q(n, j):
                a_part(n, A_Q + j, flat(qT, slice(None), slice(2 * j, 2 * j + 2), slice(None)), bank_a(A_Q + j)[:, :])

            def a_k(n):
                a_part(n, A_K, flat(kT, slice(None), slice(None), slice(None)), bank_a(A_K)[:, 0:HC * NCE])

            def a_v(n):
                a_part(n, A_V, [t[:, :, 0:D] for t in v], bank_a(A_V)[0:NC, :].rearrange("p (a b) -> p a b", a=H))

            def a_s(n, j):
                src = bank_a(A_S + j)[:, 0:HB * NCE].rearrange("p (a b) -> p a b", a=HB)[:, :, 0:NC]
                dve.wait_ge(a_fill, a_at(n, A_S + j))
                V.tensor_reduce(s_max[:, j, :], src, AX.X, ALU.max).then_inc(s_max_ready, 1)
                dve.wait_ge(s_max_ready, at(2 * NT, n, j))
                V.tensor_tensor(probs[:, j // 2, (j % 2) * HB:(j % 2 + 1) * HB, :], src,
                                s_max[:, j, :].unsqueeze(2).to_broadcast([P, HB, NC]), ALU.subtract).then_inc(a_evac, 1)

            def a_pT(n, j):
                a_part(n, A_PT[j], flat(pT, slice(None), slice((j % 2) * HB, (j % 2 + 1) * HB), slice(None)), bank_a(A_PT[j])[0:NC, :])

            def a_pv(n, j):
                src = bank_a(A_PV[j])[:, 0:HB * DV].rearrange("p (a b) -> p a b", a=HB)
                dve.wait_ge(a_fill, a_at(n, A_PV[j]))
                V.reciprocal(r_sum[:, j, :], src[:, :, D]).then_inc(r_sum_ready, 1)
                dve.wait_ge(r_sum_ready, at(2 * NT, n, j))
                V.tensor_tensor(attn[:, j // 2, :, j % 2, :], src[:, :, 0:D],
                                r_sum[:, j, :].unsqueeze(2).to_broadcast([P, HB, D]), ALU.mult).then_inc(a_evac, 1)

            def a_aT(n, t):
                a_part(n, A_AT + t, flat(aT, slice(None), t, slice(None), slice(None)), bank_a(A_AT + t)[:, :])

            def a_y(n):
                dve.wait_ge(a_fill, a_at(n, A_Y))
                dve.wait_ge(xb_ready, at(1, n, 0))
                if not (known(n) and n == 0):
                    dve.wait_ge(x2_moved, at(1, n - 1, 0))
                V.tensor_tensor(x2a[:, :, :].rearrange("p a b -> p (a b)"), bank_a(A_Y)[:, :],
                                xb[:, :, :].rearrange("p a b -> p (a b)"), ALU.add).then_inc(a_evac, 1)

            def b_xT(n):
                dve.wait_ge(b_hi, at(1, n, 0))
                V.tensor_tensor(x2T[1][:, :, :].rearrange("p a b -> p (a b)"), bank_b(B_XT)[:, :],
                                x2T[0].bitcast(F32)[:, :, :].rearrange("p a b -> p (a b)"), ALU.subtract).then_inc(b_evac, 1)

            def b_route(n):
                dve.wait_ge(b_fill, b_at(n, B_ROUTE))
                dve.wait_ge(rn_step, at(3, n, 2))
                V.scalar_tensor_tensor(z[:, 0, :], bank_b(B_ROUTE)[:, 0:E], rn[:, 2, 0:1], sig[:, :],
                                       ALU.mult, ALU.subtract).then_inc(top_ready, 1)
                V.scalar_tensor_tensor(z[:, 1, :], bank_b(B_ROUTE)[:, E:2 * E], rn[:, 2, 1:2], sig[:, :],
                                       ALU.mult, ALU.subtract).then_inc(b_evac, 1)
                dve.wait_ge(top_ready, at(3, n, 0))
                apart(dve)
                V.max(top[:, 0, :], z[:, 0, :]).then_inc(top_ready, 1)
                dve.wait_ge(b_evac, b_read(n, B_ROUTE))
                apart(dve)
                V.max(top[:, 1, :], z[:, 1, :]).then_inc(top_ready, 1)
                for t in range(NT):
                    dve.wait_ge(top_ready, at(3, n, 1 + t))
                    apart(dve)
                    V.max_index(idx[:, t, :], top[:, t, :], z[:, t, :]).then_inc(idx_ready, 1)
                dve.wait_ge(idx_ready, at(3, n, 1))
                V.tensor_copy(idxf[:, :, :], idx[:, :, :]).then_inc(idx_ready, 1)

            def b_wsum(n):
                dve.wait_ge(w_ready, at(1, n, 0))
                V.tensor_reduce(w_sum[:, 0, :], w[:, :, :], AX.X, ALU.add).then_inc(w_sum_ready, 1)
                dve.wait_ge(w_sum_ready, at(2, n, 0))
                V.reciprocal(w_sum[:, 1, :], w_sum[:, 0, :]).then_inc(w_sum_ready, 1)

            def b_qkv(n, j):
                fill, t, ep = B_QKV + j, j // EP, j % EP
                dve.wait_ge(b_fill, b_at(n, fill))
                if j == 0:
                    dve.wait_ge(rw_ready, at(1, n, 0))
                if ep == 0 and not (known(n) and n == 0):
                    dve.wait_ge(qkv_ready, at(NT, n - 1, t))
                for k in range(2):
                    e = 2 * ep + k
                    src = bank_b(fill)[:, k * QKV:(k + 1) * QKV]
                    if ep == 0:
                        V.tensor_scalar(acc[:, t, k, :], src, rw[:, t, e:e + 1], None, ALU.mult).then_inc(b_evac, 1)
                    else:
                        dve.wait_ge(b_evac, b_read(n, fill - 1) - 1 + k)
                        V.scalar_tensor_tensor(acc[:, t, k, :], src, rw[:, t, e:e + 1], acc[:, t, k, :],
                                               ALU.mult, ALU.add).then_inc(b_evac, 1)

            def c_part(n, fill, which, pair, src):
                dve.wait_ge(c_hi, at(3, n, which))
                V.tensor_tensor(pair[1], src, pair[0].bitcast(F32), ALU.subtract).then_inc(c_evac, 1)

            def c_qk(n):
                c_part(n, C_QK, 0, flat(qkT, slice(None), slice(None), slice(None)), bank_c(C_QK)[0:D, :])

            def c_s(n):
                dve.wait_ge(c_fill, c_at(n, C_S))
                apart(dve)
                for t in range(NT):
                    keys = slice(t * P, t * P + (t + 1) * P)
                    V.tensor_tensor_reduce(out=p2[:, keys], in0=bank_c(C_S)[:, keys], in1=causal[:, T - (t + 1) * P:T],
                                           scale=-SCALE, scalar=BIG, op0=ALU.add, op1=ALU.min,
                                           accum_out=m2[:, t:t + 1]).then_inc(c_evac, 1)

            def c_pT(n):
                c_part(n, C_PT, 1, flat(p2T, slice(None), slice(None), slice(None)), bank_c(C_PT)[:, 0:3 * P])

            def c_pv(n):
                dve.wait_ge(p2_ready, at(NT, n, NT - 1))
                V.reciprocal(p2_sum[:, 1, :], p2_sum[:, 0, :]).then_inc(r2_ready, 1)
                dve.wait_ge(c_fill, c_at(n, C_PV))
                dve.wait_ge(r2_ready, at(2, n, 0))
                V.tensor_scalar(attn2[:, 0, :, :], bank_c(C_PV)[:, 0:D].unsqueeze(1).to_broadcast([P, 2, D]),
                                p2_sum[:, 1, 0:1], None, ALU.mult).then_inc(r2_ready, 1)
                V.tensor_scalar(attn2[:, 1, :, :], bank_c(C_PV)[:, D:2 * D].unsqueeze(1).to_broadcast([P, 2, D]),
                                p2_sum[:, 1, 1:2], None, ALU.mult).then_inc(c_evac, 1)

            def c_aT(n):
                rows = slice(RG, 2 * RG)
                dve.wait_ge(c_hi, at(3, n, 2))
                V.tensor_tensor(rwT[rows, :], bank_c(C_AT)[rows, T:2 * T], rwT.bitcast(F32)[rows, :],
                                ALU.subtract).then_inc(c_evac, 1)

            def c_mix(n, j):
                dve.wait_ge(c_fill, c_at(n, C_RW + j))
                dve.wait_ge(aT2_ready, at(1, n, 0))
                if j == 3 and not (known(n) and n == 0):
                    dve.wait_ge(y_out, 16 * n)
                V.tensor_tensor(mix[:, 2 * j:2 * j + 2, :], bank_c(C_RW + j)[:, :].rearrange("p (a b) -> p a b", a=2),
                                aT2[:, :].unsqueeze(1).to_broadcast([P, 2, T]), ALU.mult).then_inc(c_evac, 1)

            def c_y(n):
                dve.wait_ge(c_fill, c_at(n, C_Y))
                dve.wait_ge(x2_moved, at(1, n, 0))
                V.tensor_tensor(y[:, :, :].rearrange("p a b -> p (a b)"), bank_c(C_Y)[:, :],
                                x2b[:, :, :].rearrange("p a b -> p (a b)"), ALU.add).then_inc(c_evac, 1)

            def step(i):
                h, a, b, c = i + 1, i, i - 1, i - 2

                def do(n, fn, *k):
                    if on(n):
                        fn(n, *k)

                do(c, c_qk)
                do(a, a_q, 0)
                do(c, c_s)
                do(b, b_route)
                do(a, a_q, 1)
                do(a, a_k)
                do(c, c_pT)
                do(b, b_wsum)
                do(a, a_v)
                do(c, c_pv)
                do(a, a_s, 0)
                do(a, a_s, 1)
                do(c, c_aT)
                do(b, b_qkv, 0)
                do(c, c_mix, 0)
                do(a, a_s, 2)
                do(b, b_qkv, 1)
                do(c, c_mix, 1)
                do(a, a_s, 3)
                do(b, b_qkv, 2)
                do(a, a_pT, 0)
                do(c, c_mix, 2)
                do(b, b_qkv, 3)
                do(a, a_pT, 1)
                do(c, c_mix, 3)
                do(b, b_qkv, 4)
                do(b, b_qkv, 5)
                do(a, a_pv, 0)
                do(a, a_pv, 1)
                do(h, ln1_a)
                do(a, a_pT, 2)
                do(b, b_qkv, 6)
                do(a, a_pT, 3)
                do(b, b_qkv, 7)
                do(h, ln1_b)
                do(c, c_y)
                do(a, a_pv, 2)
                do(a, a_pv, 3)
                do(b, b_qkv, 8)
                do(a, a_aT, 0)
                do(b, b_qkv, 9)
                do(a, a_aT, 1)
                do(b, b_qkv, 10)
                do(b, b_qkv, 11)
                do(a, a_y)
                do(a, ln2_a)
                do(b, b_qkv, 12)
                do(h, a_xT)
                do(b, b_qkv, 13)
                do(h, a_cT)
                do(a, ln2_b)
                do(b, b_qkv, 14)
                do(b, b_qkv, 15)
                do(a, b_xT)

            for i in range(-1, 3):
                step(i)
            with dve.Fori(3, B - 2) as i:
                step(i)
            for i in range(B - 2, B + 2):
                step(i)

        @block.gpsimd
        def _(pool):
            G = nc.gpsimd
            CHAIN = 10

            G.memset(ident[:, :], 0.0).then_inc(pool_step, 1)
            G.memset(causal[:, :], 0.0).then_inc(pool_step, 1)
            G.memset(rw_c[:, :, :], 0.0).then_inc(pool_step, 1)
            G.memset(sel_raw[:, :], 0.0).then_inc(pool_step, 1)
            G.iota(iota_i[:, :], pattern=[[1, E]], base=0, channel_multiplier=0).then_inc(pool_step, 1)
            pool.wait_ge(pool_step, 5)
            G.affine_select(out=ident[:, :], in_=ident[:, :], compare_op=ALU.not_equal, fill=1.0, base=0,
                            pattern=[[-1, P]], channel_multiplier=1).then_inc(consts, 1)
            G.affine_select(out=causal[:, :], in_=causal[:, :], compare_op=ALU.is_ge, fill=MASKED, base=P,
                            pattern=[[-1, T]], channel_multiplier=1).then_inc(pool_step, 1)
            sel_4d = sel_raw.rearrange("p (a b d) -> p a b d", a=EP, b=2)
            for k in range(2):
                if k:
                    pool.wait_ge(pool_step, 7)
                G.affine_select(out=sel_4d, in_=sel_4d, compare_op=ALU.not_equal, fill=1.0, base=-k * RG,
                                pattern=[[-2, EP], [-1, 2], [0, D]], channel_multiplier=1).then_inc(pool_step, 1)
            G.tensor_copy(iota[:, :], iota_i[:, :]).then_inc(pool_step, 1)
            pool.wait_ge(pool_step, 9)
            pool.wait_ge(sim_norm, 2)
            pool.wait_ge(consts, 4)
            G.tensor_tensor(sim_n[:, :], sim_n[:, :], expo[:, NT:NT + 1].to_broadcast([P, E]), ALU.pow).then_inc(sim_norm, 1)
            START = 9

            def chain(n, which):
                return CHAIN * n + which + 1 + START

            def ln_pow_step(k, n):
                pool.wait_ge(ln_var[k], at(k + 1, n, k))
                m = (k + 1) * NT
                src = pow_in[k][:, :, :].rearrange("p a b -> p (a b)")[:, 0:m]
                dst = pow_out[k][:, :, :].rearrange("p a b -> p (a b)")[:, 0:m]
                if not (known(n) and n == 0):
                    pool.wait_ge(ln_done[k], at(NT, n - 1, NT - 1))
                    if k == 1:
                        pool.wait_ge(rn_step, at(3, n - 1, 0))
                G.tensor_tensor(dst, src, expo[:, 0:m], ALU.pow).then_inc(ln_pow[k], 1)

            def a_xb(n):
                pool.wait_ge(x_in, 16 * (n + 1))
                if known(n) and n == 0:
                    pool.wait_ge(small_in, 48)
                else:
                    pool.wait_ge(a_evac, a_at(n - 1, A_Y))
                G.tensor_tensor(xb[:, :, :], xt[:, :, :], bo_all[:, :].unsqueeze(1).to_broadcast([P, NT, C]),
                                ALU.add).then_inc(xb_ready, 1)

            def x2_move(n):
                pool.wait_ge(a_evac, a_at(n, A_Y))
                if not (known(n) and n == 0):
                    pool.wait_ge(c_evac, c_read(n - 1, C_Y))
                apart(pool)
                G.tensor_copy(x2b[:, :, :], x2a[:, :, :]).then_inc(x2_moved, 1)

            def b_route(n):
                pool.wait_ge(idx_ready, at(3, n, 2))
                apart(pool)
                G.tensor_scalar(z_top[:, :], top[:, :, 0], 0.0, None, ALU.max).then_inc(pool_step, 1)
                G.tensor_scalar(idle[:, :], top[:, :, 0], 0.0, None, ALU.is_le).then_inc(pool_step, 1)
                G.tensor_scalar(g[:, :, :], z[:, :, :], 0.0, None, ALU.max).then_inc(pool_step, 1)
                G.tensor_scalar(act_on[:, :, :], z[:, :, :], 0.0, None, ALU.is_gt).then_inc(pool_step, 1)
                pool.wait_ge(pool_step, chain(n, 3))
                G.tensor_tensor(g[:, :, :], g[:, :, :], z_top[:, :].unsqueeze(2).to_broadcast([P, NT, E]),
                                ALU.subtract).then_inc(g_ready, 1)
                for t in range(NT):
                    G.tensor_scalar(first[:, t, :], iota[:, :], idxf[:, t, 0:1], idle[:, t:t + 1],
                                    ALU.is_equal, ALU.mult).then_inc(pool_step, 1)
                    G.tensor_scalar(second[:, t, :], iota[:, :], idxf[:, t, 1:2], idle[:, t:t + 1],
                                    ALU.is_equal, ALU.mult).then_inc(pool_step, 1)
                pool.wait_ge(pool_step, chain(n, 7))
                G.tensor_tensor(first[:, :, :], first[:, :, :], second[:, :, :], ALU.add).then_inc(pool_step, 1)
                pool.wait_ge(pool_step, chain(n, 8))
                G.tensor_tensor(act_on[:, :, :], act_on[:, :, :], first[:, :, :], ALU.add).then_inc(pool_step, 1)
                pool.wait_ge(pool_step, chain(n, 9))
                pool.wait_ge(e_ready, at(1, n, 0))
                G.tensor_tensor(w[:, :, :], w[:, :, :], act_on[:, :, :], ALU.mult).then_inc(w_ready, 1)

            def b_rw(n):
                pool.wait_ge(w_sum_ready, at(2, n, 1))
                if not (known(n) and n == 0):
                    pool.wait_ge(rw_c_ready, at(2, n - 1, 1))
                G.tensor_tensor(rw[:, :, :], w[:, :, :], w_sum[:, 1, :].unsqueeze(2).to_broadcast([P, NT, E]),
                                ALU.mult).then_inc(rw_ready, 1)

            def b_rw_copy(n):
                pool.wait_ge(rw_ready, at(1, n, 0))
                if not (known(n) and n == 0):
                    pool.wait_ge(c_fill, c_at(n - 1, C_AT))
                apart(pool)
                for k in range(2):
                    G.tensor_copy(rw_c[:, :, k * RG:k * RG + E], rw[:, :, :]).then_inc(rw_c_ready, 1)

            def b_sum(n, t):
                pool.wait_ge(b_evac, b_read(n, B_QKV + (t + 1) * EP - 1))
                if not (known(n) and n == 0):
                    pool.wait_ge(v2_ready, at(2, n - 1, 1))
                    pool.wait_ge(c_fill, c_at(n - 1, C_QK))
                G.tensor_tensor(qkv[:, t, :], acc[:, t, 0, :], acc[:, t, 1, :], ALU.add).then_inc(qkv_ready, 1)

            def c_v(n):
                pool.wait_ge(qkv_ready, at(NT, n, NT - 1))
                if not (known(n) and n == 0):
                    pool.wait_ge(c_fill, c_at(n - 1, C_PV))
                apart(pool)
                G.tensor_copy(v2[0][:, :, :], qkv[:, :, 2 * D:QKV]).then_inc(v2_ready, 1)
                pool.wait_ge(v2_ready, at(2, n, 0))
                G.tensor_tensor(v2[1][:, :, :], qkv[:, :, 2 * D:QKV], v2[0].bitcast(F32)[:, :, :], ALU.subtract).then_inc(v2_ready, 1)

            def c_mix(n, j):
                pool.wait_ge(mix_hi, at(4, n, j))
                G.tensor_tensor(mixs[1][:, 2 * j:2 * j + 2, :], mix[:, 2 * j:2 * j + 2, :],
                                mixs[0].bitcast(F32)[:, 2 * j:2 * j + 2, :], ALU.subtract).then_inc(mix_lo, 1)

            def step(i):
                h, a, b, c = i + 1, i, i - 1, i - 2

                def do(n, fn, *k):
                    if on(n):
                        fn(n, *k)

                do(c, c_v)
                do(b, b_route)
                do(b, b_rw)
                for j in range(4):
                    do(c, c_mix, j)
                do(b, b_rw_copy)
                if on(h):
                    ln_pow_step(0, h)
                do(b, b_sum, 0)
                do(b, x2_move)
                do(h, a_xb)
                if on(a):
                    ln_pow_step(1, a)
                do(b, b_sum, 1)

            for i in range(-1, 3):
                step(i)
            with pool.Fori(3, B - 2) as i:
                step(i)
            for i in range(B - 2, B + 2):
                step(i)


_INS = ['x', 'ctx_768', 'L0_xattn_Wq', 'L0_xattn_Wk', 'L0_xattn_Wv', 'L0_xattn_Wo', 'L0_xattn_bo', 'L0_ffn_sim_matrix',
        'L0_ffn_gates', 'L0_ffn_q_proj', 'L0_ffn_k_proj', 'L0_ffn_v_proj', 'L0_ffn_o_proj']


def kernel(**inputs):
    import numpy as _np
    import concourse.bacc as _bacc
    from concourse import mybir as _mybir
    from concourse.bass_utils import run_bass_kernel_spmd as _run

    nc = _bacc.Bacc("TRN2", target_bir_lowering=False, num_devices=1)
    arrays, args = {}, []
    for name in _INS:
        a = _np.ascontiguousarray(inputs[name])
        arrays[f"in_{name}_dram"] = a
        args.append(nc.dram_tensor(f"in_{name}_dram", a.shape, _mybir.dt.from_np(a.dtype), kind="ExternalInput").ap())
    shape = inputs['x'].shape
    args.append(nc.dram_tensor("out_0_dram", shape, _mybir.dt.float32, kind="ExternalOutput").ap())
    xattn_moe_kernel(nc, *args)
    r = _run(nc, [arrays], core_ids=[0])
    return r.results[0]["out_0_dram"]
```

```python
import concourse.bass as bass
from concourse import mybir
from concourse.alu_op_type import AluOpType as ALU
from contextlib import ExitStack

F32 = mybir.dt.float32
F32R = mybir.dt.float32r
U32 = mybir.dt.uint32
ACT = mybir.ActivationFunctionType
AX = mybir.AxisListType


def xattn_moe_kernel(nc, x, ctx_in, Wq, Wk, Wv, Wo, bo, sim_matrix, gates, q_proj, k_proj, v_proj, o_proj, out):
    B, T, C = x.shape
    NC, DC = ctx_in.shape[1:]
    P = 128
    NT = T // P
    CC = C // P
    INNER = Wq.shape[1]
    D = 64
    H = INNER // D
    HC = INNER // P
    NCE = NC + NC % 2
    E = sim_matrix.shape[1]
    QKV = 3 * D
    EP = E // 2
    DK = DC // 2
    RG = 32
    EPS = 1e-5
    TINY = 1e-12
    SCALE = D ** -0.5
    MASKED = -1e30
    BIG = 3e38

    A_CT, A_K, A_XT, A_V, A_KT, A_Q, A_S, A_Y = 0, 1, 2, 3, 4, 5, 7, 17
    A_PT, A_PV = (11, 12, 14, 15), (13, 16)
    A_FILLS, A_BANKS = 18, 3
    B_XT, B_QKV = 0, 2
    B_FILLS, B_BANKS = B_QKV + NT * EP, 3
    C_RT, C_QK, C_S, C_PT, C_PV, C_RW, C_Y = 0, 1, 2, 3, 4, 5, 9
    C_FILLS, C_BANKS = 10, 2
    assert A_FILLS % A_BANKS == 0 and B_FILLS % B_BANKS == 0 and C_FILLS % C_BANKS == 0
    HB = H // 2

    def a_at(n, fill):
        return A_FILLS * n + fill + 1

    def b_at(n, fill):
        return B_FILLS * n + fill + 1

    def c_at(n, fill):
        return C_FILLS * n + fill + 1

    def a_read(n, fill):
        assert fill % A_FILLS != A_K
        return (A_FILLS - 1) * n + fill + (1 if fill < A_K else 0)

    def b_read(n, fill):
        return (B_QKV + 2 * NT * EP) * n + (fill + 1 if fill < B_QKV else 2 * fill)

    def c_read(n, fill):
        return (C_FILLS + 1) * n + fill + (1 if fill < C_S else 2)

    A_HI = {fill: k for k, fill in enumerate((A_CT, A_XT, A_V, A_KT, A_Q, A_Q + 1, A_PT[0], A_PT[1], A_PV[0],
                                              A_PT[2], A_PT[3], A_PV[1]))}

    def a_hi_at(n, fill):
        return len(A_HI) * n + A_HI[fill] + 1

    def at(per_batch, n, which):
        return per_batch * n + which + 1

    def known(n):
        return isinstance(n, int)

    def on(n):
        return not known(n) or 0 <= n < B

    es = ExitStack()
    with es:
        def sb(name, shape, dt=F32):
            return es.enter_context(nc.sbuf_tensor(name, shape, dt))

        def split(name, shape):
            return sb(name + "_hi", shape, F32R), sb(name + "_lo", shape, F32R)

        def sem(name):
            return es.enter_context(nc.semaphore(name))

        wq = split("wq", [P, CC, INNER])
        wk = split("wk", [DK, 2, INNER])
        wv = split("wv", [DK, 2, INNER])
        wo = split("wo", [P, HC, C])
        wqkv = split("wqkv", [P, CC, E + E * QKV])
        wo2 = split("wo2", [P, EP, C])
        wsim = [t[:, :, 0:E] for t in wqkv]
        bo_all = sb("bo_all", [P, C])
        sig = sb("sig", [P, E])
        ident = sb("ident", [P, P])
        causal = sb("causal", [P, T])
        expo = sb("expo", [P, 2 * NT])
        iota = sb("iota", [P, E])
        xt = sb("xt", [P, NT, C])
        xb = sb("xb", [P, NT, C])
        xn = sb("xn", [P, NT, C])
        x2a = sb("x2a", [P, NT, C])
        x2b = sb("x2b", [P, NT, C])
        x2n = sb("x2n", [P, NT, C])
        stats = [sb(f"stats{k}", [P, NT, 6]) for k in (1, 2)]
        mv = [sb(f"mv{k}", [P, NT, 2]) for k in (1, 2)]
        pow_in = [sb(f"pow_in{k}", [P, 2, NT]) for k in (1, 2)]
        pow_out = [sb(f"pow_out{k}", [P, 2, NT]) for k in (1, 2)]
        rn = sb("rn", [P, 3, NT])
        ct = sb("ct", [NC, DC])
        xT = split("xT", [P, CC, T])
        cT = split("cT", [DK, 2, NCE])
        qT = split("qT", [P, HC, T])
        kT = split("kT", [P, HC, 2, NCE])
        v = split("v", [NC, HC, 3, D])
        s_max = sb("s_max", [P, 2 * NT, HB])
        probs = sb("probs", [P, NT, H, NC])
        pT = split("pT", [NC, HB, T])
        p_sum = sb("p_sum", [P, 2, 2, NT, HB])
        aT = split("aT", [P, HC, T])
        x2T = split("x2T", [P, CC, T])
        rwT = sb("rwT", [2 * RG, T], F32R)
        sel = sb("sel", [2 * RG, EP, P], F32R)
        z = sb("z", [P, NT, E])
        top = sb("top", [P, NT, 8])
        idx = sb("idx", [P, NT, 8], U32)
        idxf = sb("idxf", [P, NT, 8])
        z_top = sb("z_top", [P, NT])
        idle = sb("idle", [P, NT])
        first = sb("first", [P, NT, E])
        second = sb("second", [P, NT, E])
        act_on = sb("act_on", [P, NT, E])
        g = sb("g", [P, NT, E])
        w = sb("w", [P, NT, E])
        w_sum = sb("w_sum", [P, 2, NT])
        rw = sb("rw", [P, NT, E])
        rw_c = sb("rw_c", [P, NT, 2 * RG])
        acc = sb("acc", [P, NT, 2, QKV])
        qkv = sb("qkv", [P, NT, QKV])
        qkT = split("qkT", [D, 2, T])
        v2 = split("v2", [P, NT, 2, D])
        m2 = sb("m2", [P, NT])
        p2 = sb("p2", [P, P + T])
        p2_sum = sb("p2_sum", [P, 2, NT])
        p2T = split("p2T", [P, 3, P])
        aT2 = sb("aT2", [P, T])
        mix = sb("mix", [P, EP, T])
        mixs = split("mixs", [P, EP, T])
        y = mix[:, EP - NT:EP, :]

        banks_a = [es.enter_context(nc.psum_tensor(f"bank_a{k}", [P, 512], F32)) for k in range(A_BANKS)]
        banks_b = [es.enter_context(nc.psum_tensor(f"bank_b{k}", [P, 512], F32)) for k in range(B_BANKS)]
        banks_c = [es.enter_context(nc.psum_tensor(f"bank_c{k}", [P, 512], F32)) for k in range(C_BANKS)]

        def bank_a(fill):
            return banks_a[fill % A_BANKS]

        def bank_b(fill):
            return banks_b[fill % B_BANKS]

        def bank_c(fill):
            return banks_c[fill % C_BANKS]

        a_fill, a_hi, a_evac = sem("a_fill"), sem("a_hi"), sem("a_evac")
        b_fill, b_hi, b_evac = sem("b_fill"), sem("b_hi"), sem("b_evac")
        c_fill, c_hi, c_evac = sem("c_fill"), sem("c_hi"), sem("c_evac")
        x_in, ct_in, y_out = sem("x_in"), sem("ct_in"), sem("y_out")
        ln_stats = [sem(f"ln_stats{k}") for k in (1, 2)]
        ln_var = [sem(f"ln_var{k}") for k in (1, 2)]
        ln_pow = [sem(f"ln_pow{k}") for k in (1, 2)]
        ln_done = [sem(f"ln_done{k}") for k in (1, 2)]
        rn_step = sem("rn_step")
        k_ready = sem("k_ready")
        xb_ready, x2_moved = sem("xb_ready"), sem("x2_moved")
        s_max_ready, p_exp, p_sum_ready, p_ready = sem("s_max_ready"), sem("p_exp"), sem("p_sum_ready"), sem("p_ready")
        top_ready, idx_ready = sem("top_ready"), sem("idx_ready")
        pool_step = sem("pool_step")
        g_ready, e_ready, w_ready, w_sum_ready = sem("g_ready"), sem("e_ready"), sem("w_ready"), sem("w_sum_ready")
        rw_ready, rw_c_ready, qkv_ready, v2_ready = sem("rw_ready"), sem("rw_c_ready"), sem("qkv_ready"), sem("v2_ready")
        p2_exp, p2_sum_ready, p2_ready = sem("p2_exp"), sem("p2_sum_ready"), sem("p2_ready")
        mix_hi, mix_lo = sem("mix_hi"), sem("mix_lo")
        consts, wt_in, wt_hi, wt_ready = sem("consts"), [sem("wt_in0"), sem("wt_in1")], sem("wt_hi"), sem("wt_ready")
        small_in, sig_step, sim_step, sim_norm = sem("small_in"), sem("sig_step"), sem("sim_step"), sem("sim_norm")
        pad_done = sem("pad_done")
        passed = sem("passed")

        setup = acc[:, :, :, :].rearrange("p a b c -> p (a b c)")
        ones = setup[:, 0:P]
        sim_raw, sim_sq = [setup[:, P + k * CC * E:P + (k + 1) * CC * E].rearrange("p (a b) -> p a b", a=CC) for k in range(2)]
        sim_n, half_e, iota_i = [setup[:, P + (2 * CC + k) * E:P + (2 * CC + k + 1) * E] for k in range(3)]
        iota_i = iota_i.bitcast(mybir.dt.int32)
        k_rows = probs[:, :, :, :].rearrange("p a b c -> p (a b c)")[0:NC, 0:INNER]
        sel_raw = probs[:, :, :, :].rearrange("p a b c -> p (a b c)")[0:2 * RG, 0:EP * P]
        def apart(eng):
            eng.sem_inc(passed, 1)

        SP_COLS = EP * T // 2
        stage = [mix[:, k * EP // 2:(k + 1) * EP // 2, :].rearrange("p a b -> p (a b)") for k in range(2)]
        E4 = E // 4

        def proj_piece(cc, quarter):
            e0, e1 = quarter * E4, (quarter + 1) * E4
            loads = [(lambda s, k=k: s[:, 0:E4 * QKV].rearrange("p (e f) -> p e f", f=QKV)[:, :, k * D:(k + 1) * D],
                      w_[e0:e1, cc * P:(cc + 1) * P, :].rearrange("e c d -> c e d"))
                     for k, w_ in enumerate((q_proj, k_proj, v_proj))]
            return loads, E4 * QKV, P, [t[:, cc, E + e0 * QKV:E + e1 * QKV] for t in wqkv]

        def chunked_piece(dst, src, n):
            rows, cols = src.shape[0], src.shape[2]
            return ([(lambda s: s[0:rows, 0:n * cols].rearrange("p (a b) -> p a b", a=n), src)], n * cols, rows,
                    [t.rearrange("p a b -> p (a b)") for t in dst])

        wo2_rows = o_proj.rearrange("(a e) d b -> (e d) a b", e=2)
        PIECES = [
            chunked_piece([t[:, :, :] for t in wq], Wq.rearrange("(a p) b -> p a b", p=P), CC),
            chunked_piece([t[:, :, :] for t in wk], Wk.rearrange("(a p) b -> p a b", p=DK), 2),
            chunked_piece([t[:, :, :] for t in wv], Wv.rearrange("(a p) b -> p a b", p=DK), 2),
            chunked_piece([t[:, :, :] for t in wo], Wo.rearrange("(a p) b -> p a b", p=P), HC),
            *[proj_piece(cc, quarter) for quarter in range(4) for cc in range(CC)],
            *[chunked_piece([t[:, k * EP // 2:(k + 1) * EP // 2, :] for t in wo2],
                            wo2_rows[:, k * EP // 2:(k + 1) * EP // 2, :], EP // 2) for k in range(2)],
        ]
        W_Q, W_K, W_V, W_O, W_QKV, W_O2 = 0, 1, 2, 3, (5, 7, 9, 11), 13
        assert len(PIECES) == W_O2 + 1 and all(cols <= SP_COLS for _, cols, _, _ in PIECES)

        def loads_before(piece, slot):
            return sum(len(PIECES[k][0]) for k in range(slot, piece + 1, 2))

        block = es.enter_context(nc.Block())

        @block.sync
        def _(sp):
            def load_x(n):
                if not (known(n) and n == 0):
                    sp.wait_ge(xb_ready, at(1, n - 1, 0))
                    sp.wait_ge(ln_done[0], at(NT, n - 1, NT - 1))
                sp.dma_start(xt[:, :, :], x[n, :, :].rearrange("(t p) c -> p t c", p=P)).then_inc(x_in, 16)

            def load_ctx(n):
                if not (known(n) and n == 0):
                    sp.wait_ge(a_fill, a_at(n - 1, A_CT))
                sp.dma_start(ct[:, :], ctx_in[n, :, :]).then_inc(ct_in, 16)

            def store(n):
                sp.wait_ge(c_evac, c_read(n, C_Y))
                sp.dma_start(out[n, :, :].rearrange("(t p) c -> p t c", p=P), y[:, :, :]).then_inc(y_out, 16)

            load_x(0)
            load_ctx(0)
            sp.dma_start(sim_raw[:, :, :], sim_matrix.rearrange("(a p) e -> p a e", p=P)).then_inc(small_in, 16)
            sp.dma_start(sig[:, :], gates.partition_broadcast(P)).then_inc(small_in, 16)
            sp.dma_start(bo_all[:, :], bo.partition_broadcast(P)).then_inc(small_in, 16)
            for k, (loads, cols, rows, dst) in enumerate(PIECES):
                if k >= 2:
                    sp.wait_ge(wt_ready, k - 1)
                for view, src in loads:
                    sp.dma_start(view(stage[k % 2]), src).then_inc(wt_in[k % 2], 16)

            def step(i):
                if on(i + 2):
                    load_ctx(i + 2)
                if on(i - 2):
                    store(i - 2)
                if on(i + 2):
                    load_x(i + 2)

            for i in range(-1, 3):
                step(i)
            with sp.Fori(3, B - 2) as i:
                step(i)
            for i in range(B - 2, B + 2):
                step(i)
            sp.wait_ge(y_out, 16 * B)

        @block.tensor
        def _(pe):
            def product(dst, lhs, rhs, start=True, stop=True):
                nc.tensor.matmul(dst, lhs[1], rhs[0], start=start, stop=False)
                nc.tensor.matmul(dst, lhs[0], rhs[1], start=False, stop=False)
                return nc.tensor.matmul(dst, lhs[0], rhs[0], start=False, stop=stop)

            def part(pair, *at_):
                return [t[at_] for t in pair]

            def ring_a(n, fill):
                if fill - A_BANKS == A_K:
                    pe.wait_ge(k_ready, at(1, n, 0))
                elif fill >= A_BANKS:
                    pe.wait_ge(a_evac, a_read(n, fill - A_BANKS))
                elif not (known(n) and n == 0):
                    pe.wait_ge(a_evac, a_read(n - 1, fill - A_BANKS + A_FILLS))

            def ring_b(n, fill):
                if not (known(n) and n == 0 and fill < B_BANKS):
                    if fill >= B_BANKS:
                        pe.wait_ge(b_evac, b_read(n, fill - B_BANKS))
                    else:
                        pe.wait_ge(b_evac, b_read(n - 1, fill - B_BANKS + B_FILLS))

            def ring_c(n, fill):
                if not (known(n) and n == 0 and fill < C_BANKS):
                    if fill >= C_BANKS:
                        pe.wait_ge(c_evac, c_read(n, fill - C_BANKS))
                    else:
                        pe.wait_ge(c_evac, c_read(n - 1, fill - C_BANKS + C_FILLS))

            def weights(n, piece):
                if known(n) and n == 0:
                    pe.wait_ge(wt_ready, piece + 1)

            def a_xT(n):
                ring_a(n, A_XT)
                pe.wait_ge(ln_done[0], at(NT, n, NT - 1))
                for cc in range(CC):
                    for t in range(NT):
                        last = nc.tensor.transpose(bank_a(A_XT)[:, cc * T + t * P:cc * T + (t + 1) * P],
                                                   xn[:, t, cc * P:(cc + 1) * P], ident[:, :])
                last.then_inc(a_fill, 1)

            def a_cT(n):
                ring_a(n, A_CT)
                pe.wait_ge(ct_in, 16 * (n + 1))
                for k in range(2):
                    last = nc.tensor.transpose(bank_a(A_CT)[0:DK, k * P:k * P + NC], ct[:, k * DK:(k + 1) * DK],
                                               ident[0:NC, 0:NC])
                last.then_inc(a_fill, 1)

            def a_q(n, j):
                fill = A_Q + j
                ring_a(n, fill)
                weights(n, W_Q)
                pe.wait_ge(a_evac, a_read(n, A_XT))
                for k in range(2):
                    hc = 2 * j + k
                    for cc in range(CC):
                        last = product(bank_a(fill)[:, k * T:(k + 1) * T],
                                       part(wq, slice(None), cc, slice(hc * P, (hc + 1) * P)),
                                       part(xT, slice(None), cc, slice(None)), cc == 0, cc == CC - 1)
                last.then_inc(a_fill, 1)

            def a_k(n):
                ring_a(n, A_K)
                weights(n, W_K)
                pe.wait_ge(a_evac, a_read(n, A_CT))
                for k in range(2):
                    last = product(bank_a(A_K)[0:NC, :], part(cT, slice(None), k, slice(0, NC)),
                                   part(wk, slice(None), k, slice(None)), k == 0, k == 1)
                last.then_inc(a_fill, 1)

            def a_v(n):
                ring_a(n, A_V)
                weights(n, W_V)
                for k in range(2):
                    last = product(bank_a(A_V)[0:NC, :], part(cT, slice(None), k, slice(0, NC)),
                                   part(wv, slice(None), k, slice(None)), k == 0, k == 1)
                last.then_inc(a_fill, 1)

            def a_kT(n):
                ring_a(n, A_KT)
                pe.wait_ge(k_ready, at(1, n, 0))
                for hc in range(HC):
                    last = nc.tensor.transpose(bank_a(A_KT)[:, hc * NCE:hc * NCE + NC], k_rows[:, hc * P:(hc + 1) * P],
                                               ident[0:NC, 0:NC])
                last.then_inc(a_fill, 1)

            def a_s(n, j):
                fill, half, t = A_S + j, j // 2, j % 2
                ring_a(n, fill)
                if known(n) and n == 0:
                    pe.wait_ge(pad_done, 4)
                pe.wait_ge(a_evac, a_read(n, A_Q + half))
                for k in range(2):
                    hc = 2 * half + k
                    last = product(bank_a(fill)[:, k * 2 * NCE:(k + 1) * 2 * NCE],
                                   part(qT, slice(None), hc, slice(t * P, (t + 1) * P)),
                                   [w_[:, hc, :, :].rearrange("p a b -> p (a b)") for w_ in kT])
                last.then_inc(a_fill, 1)

            def a_pT(n, j):
                fill, half, t = A_PT[j], j // 2, j % 2
                ring_a(n, fill)
                pe.wait_ge(p_ready, at(2, n, half))
                for k in range(HB):
                    last = nc.tensor.transpose(bank_a(fill)[0:NC, k * P:(k + 1) * P], probs[:, t, half * HB + k, :], ident[:, :])
                last.then_inc(a_fill, 1)

            def a_pv(n, half):
                fill = A_PV[half]
                ring_a(n, fill)
                pe.wait_ge(a_evac, a_read(n, A_PT[2 * half + 1]))
                for k in range(2):
                    hc = 2 * half + k
                    for odd in range(2):
                        last = product(bank_a(fill)[:, k * T:(k + 1) * T],
                                       [w_[:, hc, odd:odd + 2, :].rearrange("p a b -> p (a b)") for w_ in v],
                                       part(pT, slice(None), 2 * k + odd, slice(None)), odd == 0, odd == 1)
                last.then_inc(a_fill, 1)

            def a_y(n):
                ring_a(n, A_Y)
                weights(n, W_O)
                pe.wait_ge(a_evac, a_read(n, A_PV[1]))
                for t in range(NT):
                    for hc in range(HC):
                        last = product(bank_a(A_Y)[:, t * C:(t + 1) * C], part(aT, slice(None), hc, slice(t * P, (t + 1) * P)),
                                       part(wo, slice(None), hc, slice(None)), hc == 0, hc == HC - 1)
                last.then_inc(a_fill, 1)

            def b_xT(n, t):
                ring_b(n, B_XT + t)
                pe.wait_ge(ln_done[1], at(NT, n, NT - 1))
                for cc in range(CC):
                    last = nc.tensor.transpose(bank_b(B_XT + t)[:, cc * P:(cc + 1) * P],
                                               x2n[:, t, cc * P:(cc + 1) * P], ident[:, :])
                last.then_inc(b_fill, 1)

            def b_qkv(n, j):
                fill, ep, t = B_QKV + j, j // NT, j % NT
                ring_b(n, fill)
                weights(n, W_QKV[ep * 2 // E4])
                if ep == 0:
                    if known(n) and n == 0:
                        pe.wait_ge(sim_step, 6)
                    pe.wait_ge(b_evac, b_read(n, B_XT + t))
                lo = 0 if ep == 0 else E + 2 * ep * QKV
                cols = slice(lo, E + 2 * (ep + 1) * QKV)
                for cc in range(CC):
                    last = product(bank_b(fill)[:, 0:cols.stop - lo], part(x2T, slice(None), cc, slice(t * P, (t + 1) * P)),
                                   part(wqkv, slice(None), cc, cols), cc == 0, cc == CC - 1)
                last.then_inc(b_fill, 1)

            def c_qk(n):
                ring_c(n, C_QK)
                pe.wait_ge(qkv_ready, at(NT, n, NT - 1))
                apart(pe)
                for k in range(2):
                    for t in range(NT):
                        last = nc.tensor.transpose(bank_c(C_QK)[0:D, k * T + t * P:k * T + (t + 1) * P],
                                                   qkv[:, t, k * D:(k + 1) * D], ident[:, :])
                last.then_inc(c_fill, 1)

            def c_s(n):
                ring_c(n, C_S)
                pe.wait_ge(c_evac, c_read(n, C_QK))
                for t in range(NT):
                    keys = (t + 1) * P
                    last = product(bank_c(C_S)[:, t * P:t * P + keys], part(qkT, slice(None), 0, slice(t * P, (t + 1) * P)),
                                   part(qkT, slice(None), 1, slice(0, keys)))
                last.then_inc(c_fill, 1)

            def c_pT(n):
                ring_c(n, C_PT)
                pe.wait_ge(p2_ready, at(NT, n, NT - 1))
                for k in range(3):
                    last = nc.tensor.transpose(bank_c(C_PT)[:, k * P:(k + 1) * P], p2[:, k * P:(k + 1) * P], ident[:, :])
                last.then_inc(c_fill, 1)

            def c_rT(n):
                ring_c(n, C_RT)
                pe.wait_ge(rw_c_ready, at(2, n, 1))
                apart(pe)
                for t in range(NT):
                    last = nc.tensor.transpose(bank_c(C_RT)[0:2 * RG, t * P:(t + 1) * P], rw_c[:, t, :], ident[:, :])
                last.then_inc(c_fill, 1)

            def c_pv(n):
                ring_c(n, C_PV)
                pe.wait_ge(c_evac, c_read(n, C_PT))
                pe.wait_ge(v2_ready, at(2, n, 1))
                vs = [[w_[:, t, :, :].rearrange("p a b -> p (a b)") for w_ in v2] for t in range(NT)]
                product(bank_c(C_PV)[:, 0:T], vs[0], [w_[:, 0:2, :].rearrange("p a b -> p (a b)") for w_ in p2T], True, False)
                product(bank_c(C_PV)[:, P:T], vs[1], part(p2T, slice(None), 2, slice(None)), False, True).then_inc(c_fill, 1)

            def c_rw(n, j):
                fill = C_RW + j
                ring_c(n, fill)
                pe.wait_ge(c_evac, c_read(n, C_RT))
                for k in range(2):
                    last = nc.tensor.matmul(bank_c(fill)[:, k * T:(k + 1) * T], sel[:, 2 * j + k, :], rwT[:, :],
                                            start=True, stop=True)
                last.then_inc(c_fill, 1)

            def c_y(n, quarter):
                t, half = quarter // 2, quarter % 2
                if quarter == 0:
                    ring_c(n, C_Y)
                    weights(n, W_O2)
                for ep in range(half * EP // 2, (half + 1) * EP // 2):
                    if t == 0 and ep % 2 == 0:
                        pe.wait_ge(mix_lo, at(4, n, ep // 2))
                    last = product(bank_c(C_Y)[:, t * C:(t + 1) * C],
                                   part(mixs, slice(None), ep, slice(t * P, (t + 1) * P)),
                                   part(wo2, slice(None), ep, slice(None)), ep == 0, ep == EP - 1)
                if quarter == 3:
                    last.then_inc(c_fill, 1)

            def sim_norms():
                pe.wait_ge(consts, 4)
                pe.wait_ge(sim_step, 1)
                for cc in range(CC):
                    last = nc.tensor.matmul(bank_b(0)[:, 0:E], ones[:, :], sim_sq[:, cc, :], start=cc == 0, stop=cc == CC - 1)
                last.then_inc(sim_norm, 1)

            sim_norms()

            def step(i):
                ahead, now, before, before2 = i + 1, i, i - 1, i - 2

                def do(n, fn, *k):
                    if on(n):
                        fn(n, *k)

                do(before, a_pv, 1)
                do(before2, b_qkv, 12)
                do(before2, b_qkv, 13)
                do(before, a_y)
                do(now, a_cT)
                do(before2, b_qkv, 14)
                do(before2, b_qkv, 15)
                do(now, a_k)
                do(now, a_xT)
                do(now, a_v)
                do(before, b_xT, 0)
                do(before2, c_rT)
                do(before2, c_qk)
                do(before, b_xT, 1)
                do(now, a_kT)
                do(before, b_qkv, 0)
                do(before2, c_s)
                do(before, b_qkv, 1)
                do(now, a_q, 0)
                do(now, a_q, 1)
                do(before2, c_pT)
                do(before, b_qkv, 2)
                do(now, a_s, 0)
                do(before2, c_pv)
                do(before2, c_rw, 0)
                do(now, a_s, 1)
                do(before2, c_rw, 1)
                do(now, a_s, 2)
                do(now, a_s, 3)
                do(before2, c_rw, 2)
                do(before, b_qkv, 3)
                do(before2, c_rw, 3)
                do(before, b_qkv, 4)
                do(before, b_qkv, 5)
                do(before2, c_y, 0)
                do(before, b_qkv, 6)
                do(before, b_qkv, 7)
                do(before2, c_y, 1)
                do(before2, c_y, 2)
                do(now, a_pT, 0)
                do(now, a_pT, 1)
                do(before2, c_y, 3)
                do(before, b_qkv, 8)
                do(now, a_pv, 0)
                do(before, b_qkv, 9)
                do(now, a_pT, 2)
                do(now, a_pT, 3)
                do(before, b_qkv, 10)
                do(before, b_qkv, 11)

            for i in range(-1, 3):
                step(i)
            with pe.Fori(3, B - 2) as i:
                step(i)
            for i in range(B - 2, B + 2):
                step(i)

        @block.scalar
        def _(act):
            copy = ACT.Copy

            act.wait_ge(small_in, 48)
            nc.scalar.activation(half_e[:, :], sig[:, :], ACT.Exp, scale=-1.0).then_inc(sig_step, 1)
            for k, (loads, cols, rows, dst) in enumerate(PIECES):
                act.wait_ge(wt_in[k % 2], 16 * loads_before(k, k % 2))
                nc.scalar.activation(dst[0], stage[k % 2][0:rows, 0:cols], copy).then_inc(wt_hi, 1)

            def a_part(n, fill, dst, src):
                act.wait_ge(a_fill, a_at(n, fill))
                nc.scalar.activation(dst, src, copy).then_inc(a_hi, 1)

            def a_xT(n):
                a_part(n, A_XT, xT[0][:, :, :].rearrange("p a b -> p (a b)"), bank_a(A_XT)[:, :])

            def a_cT(n):
                if known(n) and n == 0:
                    act.wait_ge(pad_done, 2)
                src = bank_a(A_CT)[0:DK, 0:2 * P].rearrange("p (a b) -> p a b", a=2)
                a_part(n, A_CT, cT[0][:, :, 0:NC], src[:, :, 0:NC])

            def a_q(n, j):
                a_part(n, A_Q + j, qT[0][:, 2 * j:2 * j + 2, :].rearrange("p a b -> p (a b)"), bank_a(A_Q + j)[:, :])

            def a_k(n):
                act.wait_ge(a_fill, a_at(n, A_K))
                nc.scalar.activation(k_rows, bank_a(A_K)[0:NC, :], copy).then_inc(k_ready, 1)

            def a_v(n):
                if known(n) and n == 0:
                    act.wait_ge(pad_done, 4)
                a_part(n, A_V, v[0][:, :, 0:3:2, :], bank_a(A_V)[0:NC, :].rearrange("p (a b c) -> p a b c", a=HC, b=2))

            def a_kT(n):
                act.wait_ge(a_fill, a_at(n, A_KT))
                for k in range(2):
                    rows = slice(k * D, (k + 1) * D)
                    src = bank_a(A_KT)[rows, 0:HC * NCE].rearrange("p (a b) -> p a b", a=HC)[:, :, 0:NC]
                    last = nc.scalar.activation(kT[0][rows, :, k, 0:NC], src, copy)
                last.then_inc(a_hi, 1)

            def a_exp(n, j):
                half, t = j // 2, j % 2
                act.wait_ge(a_evac, a_read(n, A_S + j))
                nc.scalar.activation(probs[:, t, half * HB:(half + 1) * HB, :], probs[:, t, half * HB:(half + 1) * HB, :],
                                     ACT.Exp, scale=SCALE).then_inc(p_exp, 1)

            def a_pT(n, j):
                t = j % 2
                a_part(n, A_PT[j], pT[0][:, :, t * P:(t + 1) * P], bank_a(A_PT[j])[0:NC, :].rearrange("p (a b) -> p a b", a=HB))

            def a_pv(n, half):
                a_part(n, A_PV[half], aT[0][:, 2 * half:2 * half + 2, :].rearrange("p a b -> p (a b)"), bank_a(A_PV[half])[:, :])

            def b_xT(n, t):
                act.wait_ge(b_fill, b_at(n, B_XT + t))
                nc.scalar.activation(x2T[0][:, :, t * P:(t + 1) * P], bank_b(B_XT + t)[:, 0:CC * P].rearrange("p (a b) -> p a b", a=CC),
                                     copy).then_inc(b_hi, 1)

            def b_exp(n):
                act.wait_ge(g_ready, at(1, n, 0))
                nc.scalar.activation(w[:, :, :], g[:, :, :], ACT.Exp).then_inc(e_ready, 1)

            def c_part(n, fill, dst, src):
                act.wait_ge(c_fill, c_at(n, fill))
                nc.scalar.activation(dst, src, copy).then_inc(c_hi, 1)

            def c_qk(n):
                c_part(n, C_QK, qkT[0][:, :, :].rearrange("p a b -> p (a b)"), bank_c(C_QK)[0:D, :])

            def c_exp(n):
                for t in range(NT):
                    keys = slice(t * P, t * P + (t + 1) * P)
                    act.wait_ge(c_evac, c_read(n, C_S) - NT + 1 + t)
                    nc.scalar.activation(p2[:, keys], p2[:, keys], ACT.Exp, bias=m2[:, t:t + 1], scale=-1.0,
                                         accum_out=p2_sum[:, 0, t:t + 1]).then_inc(p2_exp, 1)

            def c_pT(n):
                c_part(n, C_PT, p2T[0][:, :, :].rearrange("p a b -> p (a b)"), bank_c(C_PT)[:, 0:3 * P])

            def c_rT(n):
                c_part(n, C_RT, rwT[:, :], bank_c(C_RT)[0:2 * RG, 0:T])

            def c_pv(n):
                act.wait_ge(c_fill, c_at(n, C_PV))
                nc.scalar.activation(aT2[:, :], bank_c(C_PV)[:, 0:T], copy).then_inc(c_evac, 1)

            def c_mix(n, j):
                act.wait_ge(c_evac, c_read(n, C_RW + j))
                nc.scalar.activation(mixs[0][:, 2 * j:2 * j + 2, :], mix[:, 2 * j:2 * j + 2, :], copy).then_inc(mix_hi, 1)

            def step(i):
                ahead, now, before, before2 = i + 1, i, i - 1, i - 2

                def do(n, fn, *k):
                    if on(n):
                        fn(n, *k)

                do(before, a_pT, 3)
                do(before, a_pv, 1)
                do(now, a_cT)
                do(now, a_k)
                do(now, a_xT)
                do(before, b_xT, 0)
                do(before2, c_rT)
                do(before2, c_qk)
                do(before, b_xT, 1)
                do(now, a_v)
                do(now, a_kT)
                do(before2, c_exp)
                do(now, a_q, 0)
                do(now, a_q, 1)
                do(before2, c_pT)
                do(before, b_exp)
                do(before2, c_pv)
                do(now, a_exp, 0)
                do(before2, c_mix, 0)
                do(before2, c_mix, 1)
                do(before2, c_mix, 2)
                do(before2, c_mix, 3)
                do(now, a_exp, 1)
                do(now, a_pT, 0)
                do(now, a_pT, 1)
                do(now, a_exp, 2)
                do(now, a_exp, 3)
                do(now, a_pv, 0)
                do(now, a_pT, 2)

            for i in range(-1, 3):
                step(i)
            with act.Fori(3, B - 2) as i:
                step(i)
            for i in range(B - 2, B + 2):
                step(i)

        @block.vector
        def _(dve):
            V = nc.vector

            V.memset(expo[:, 0:NT], -0.5).then_inc(consts, 1)
            V.memset(expo[:, NT:2 * NT], 0.5).then_inc(consts, 1)
            V.memset(ones[:, :], 1.0).then_inc(consts, 1)
            for k in range(2):
                V.memset(cT[k].bitcast(F32)[:, :, NC:NCE], 0.0).then_inc(pad_done, 1)
            for k in range(2):
                V.memset(v[k].bitcast(F32)[:, :, :, :], 0.0)
                V.memset(kT[k].bitcast(F32)[:, :, :, :], 0.0).then_inc(pad_done, 1)
            dve.wait_ge(small_in, 48)
            V.tensor_tensor(sim_sq[:, :, :], sim_raw[:, :, :], sim_raw[:, :, :], ALU.mult).then_inc(sim_step, 1)
            dve.wait_ge(sim_norm, 1)
            V.tensor_copy(sim_n[:, :], bank_b(0)[:, 0:E]).then_inc(sim_norm, 1)
            dve.wait_ge(sim_norm, 3)
            V.tensor_scalar(sim_n[:, :], sim_n[:, :], TINY, None, ALU.max).then_inc(sim_norm, 1)
            dve.wait_ge(sim_norm, 4)
            V.reciprocal(sim_n[:, :], sim_n[:, :]).then_inc(sim_step, 1)
            dve.wait_ge(sim_step, 2)
            V.tensor_tensor(sim_sq[:, :, :], sim_raw[:, :, :], sim_n[:, :].unsqueeze(1).to_broadcast([P, CC, E]),
                            ALU.mult).then_inc(sim_step, 1)
            dve.wait_ge(sim_step, 3)
            V.tensor_copy(wsim[0][:, :, :], sim_sq[:, :, :]).then_inc(sim_step, 1)
            dve.wait_ge(sim_step, 4)
            V.tensor_tensor(wsim[1][:, :, :], sim_sq[:, :, :], wsim[0].bitcast(F32)[:, :, :], ALU.subtract).then_inc(sim_step, 1)
            dve.wait_ge(sig_step, 1)
            V.tensor_scalar(half_e[:, :], half_e[:, :], 1.0, None, ALU.add).then_inc(sig_step, 1)
            dve.wait_ge(sig_step, 2)
            V.reciprocal(sig[:, :], half_e[:, :]).then_inc(sig_step, 1)
            dve.wait_ge(pool_step, 8)
            V.tensor_copy(sel[:, :, :].rearrange("p a b -> p (a b)"), sel_raw).then_inc(sim_step, 1)
            for k, (loads, cols, rows, dst) in enumerate(PIECES):
                dve.wait_ge(wt_hi, k + 1)
                V.tensor_tensor(dst[1], stage[k % 2][0:rows, 0:cols], dst[0].bitcast(F32), ALU.subtract).then_inc(wt_ready, 1)

            def ln_a(k, n, src):
                for t in range(NT):
                    V.bn_stats(stats[k][:, t, :], src[:, t, :]).then_inc(ln_stats[k], 1)
                for t in range(NT):
                    dve.wait_ge(ln_stats[k], at(2 * NT, n, t))
                    apart(dve)
                    V.bn_aggr(mv[k][:, t, :], stats[k][:, t, :]).then_inc(ln_stats[k], 1)
                dve.wait_ge(ln_stats[k], at(2 * NT, n, 2 * NT - 1))
                if k == 0:
                    V.tensor_scalar(pow_in[k][:, 0, :], mv[k][:, :, 1], EPS, None, ALU.add).then_inc(ln_var[k], 1)
                else:
                    V.tensor_scalar(pow_in[k][:, 0, :], mv[k][:, :, 1], EPS, None, ALU.add).then_inc(ln_var[k], 1)
                    V.tensor_scalar(pow_in[k][:, 1, :], mv[k][:, :, 1], float(C), None, ALU.mult).then_inc(ln_var[k], 1)

            def ln_b(k, n, src, dst):
                dve.wait_ge(ln_pow[k], at(1, n, 0))
                for t in range(NT):
                    V.tensor_scalar(dst[:, t, :], src[:, t, :], mv[k][:, t, 0:1], pow_out[k][:, 0, t:t + 1],
                                    ALU.subtract, ALU.mult).then_inc(ln_done[k], 1)

            def ln1_a(n):
                dve.wait_ge(x_in, 16 * (n + 1))
                ln_a(0, n, xt)

            def ln1_b(n):
                if not (known(n) and n == 0):
                    dve.wait_ge(a_fill, a_at(n - 1, A_XT))
                ln_b(0, n, xt, xn)

            def ln2_a(n):
                dve.wait_ge(a_evac, a_read(n, A_Y))
                ln_a(1, n, x2a)

            def ln2_b(n):
                if not (known(n) and n == 0):
                    dve.wait_ge(b_fill, b_at(n - 1, B_XT))
                ln_b(1, n, x2a, x2n)
                V.tensor_tensor(rn[:, 0, :], pow_out[1][:, 0, :], pow_out[1][:, 1, :], ALU.mult).then_inc(rn_step, 1)
                dve.wait_ge(rn_step, at(3, n, 0))
                V.tensor_scalar(rn[:, 1, :], rn[:, 0, :], TINY, None, ALU.max).then_inc(rn_step, 1)
                dve.wait_ge(rn_step, at(3, n, 1))
                V.reciprocal(rn[:, 2, :], rn[:, 1, :]).then_inc(rn_step, 1)

            def a_part(n, fill, pair, src):
                dve.wait_ge(a_hi, a_hi_at(n, fill))
                V.tensor_tensor(pair[1], src, pair[0].bitcast(F32), ALU.subtract).then_inc(a_evac, 1)

            def flat(pair, *at_):
                return [t[at_].rearrange("p a b -> p (a b)") for t in pair]

            def a_xT(n):
                a_part(n, A_XT, flat(xT, slice(None), slice(None), slice(None)), bank_a(A_XT)[:, :])

            def a_cT(n):
                src = bank_a(A_CT)[0:DK, 0:2 * P].rearrange("p (a b) -> p a b", a=2)
                a_part(n, A_CT, [t[:, :, 0:NC] for t in cT], src[:, :, 0:NC])

            def a_q(n, j):
                a_part(n, A_Q + j, flat(qT, slice(None), slice(2 * j, 2 * j + 2), slice(None)), bank_a(A_Q + j)[:, :])

            def a_v(n):
                a_part(n, A_V, [w_[:, :, 0:3:2, :] for w_ in v],
                       bank_a(A_V)[0:NC, :].rearrange("p (a b c) -> p a b c", a=HC, b=2))

            def a_kT(n):
                dve.wait_ge(a_hi, a_hi_at(n, A_KT))
                for k in range(2):
                    rows = slice(k * D, (k + 1) * D)
                    src = bank_a(A_KT)[rows, 0:HC * NCE].rearrange("p (a b) -> p a b", a=HC)[:, :, 0:NC]
                    last = V.tensor_tensor(kT[1][rows, :, k, 0:NC], src, kT[0].bitcast(F32)[rows, :, k, 0:NC], ALU.subtract)
                last.then_inc(a_evac, 1)

            def a_s(n, j):
                half, t = j // 2, j % 2
                src = bank_a(A_S + j)[:, 0:HB * NCE].rearrange("p (a b) -> p a b", a=HB)[:, :, 0:NC]
                dve.wait_ge(a_fill, a_at(n, A_S + j))
                V.tensor_reduce(s_max[:, j, :], src, AX.X, ALU.max).then_inc(s_max_ready, 1)
                dve.wait_ge(s_max_ready, at(2 * NT, n, j))
                V.tensor_tensor(probs[:, t, half * HB:(half + 1) * HB, :], src,
                                s_max[:, j, :].unsqueeze(2).to_broadcast([P, HB, NC]), ALU.subtract).then_inc(a_evac, 1)

            def a_psum(n, half):
                dve.wait_ge(p_exp, at(2 * NT, n, 2 * half + 1))
                V.tensor_reduce(p_sum[:, half, 0, :, :], probs[:, :, half * HB:(half + 1) * HB, :], AX.X,
                                ALU.add).then_inc(p_sum_ready, 1)
                dve.wait_ge(p_sum_ready, at(4, n, 2 * half))
                V.reciprocal(p_sum[:, half, 1, :, :], p_sum[:, half, 0, :, :]).then_inc(p_sum_ready, 1)

            def a_pT(n, j):
                t = j % 2
                a_part(n, A_PT[j], [w_[:, :, t * P:(t + 1) * P] for w_ in pT],
                       bank_a(A_PT[j])[0:NC, :].rearrange("p (a b) -> p a b", a=HB))

            def a_pv(n, half):
                a_part(n, A_PV[half], flat(aT, slice(None), slice(2 * half, 2 * half + 2), slice(None)), bank_a(A_PV[half])[:, :])

            def a_y(n):
                dve.wait_ge(a_fill, a_at(n, A_Y))
                dve.wait_ge(xb_ready, at(1, n, 0))
                if not (known(n) and n == 0):
                    dve.wait_ge(x2_moved, at(1, n - 1, 0))
                V.tensor_tensor(x2a[:, :, :].rearrange("p a b -> p (a b)"), bank_a(A_Y)[:, :],
                                xb[:, :, :].rearrange("p a b -> p (a b)"), ALU.add).then_inc(a_evac, 1)

            def b_xT(n, t):
                dve.wait_ge(b_hi, at(NT, n, t))
                V.tensor_tensor(x2T[1][:, :, t * P:(t + 1) * P], bank_b(B_XT + t)[:, 0:CC * P].rearrange("p (a b) -> p a b", a=CC),
                                x2T[0].bitcast(F32)[:, :, t * P:(t + 1) * P], ALU.subtract).then_inc(b_evac, 1)

            def b_route(n):
                dve.wait_ge(rn_step, at(3, n, 2))
                for t in range(NT):
                    dve.wait_ge(b_fill, b_at(n, B_QKV + t))
                    V.scalar_tensor_tensor(z[:, t, :], bank_b(B_QKV + t)[:, 0:E], rn[:, 2, t:t + 1], sig[:, :],
                                           ALU.mult, ALU.subtract).then_inc(top_ready, 1)
                for t in range(NT):
                    dve.wait_ge(top_ready, at(4, n, t))
                    apart(dve)
                    V.max(top[:, t, :], z[:, t, :]).then_inc(top_ready, 1)
                for t in range(NT):
                    dve.wait_ge(top_ready, at(4, n, 2 + t))
                    apart(dve)
                    V.max_index(idx[:, t, :], top[:, t, :], z[:, t, :]).then_inc(idx_ready, 1)
                dve.wait_ge(idx_ready, at(3, n, 1))
                V.tensor_copy(idxf[:, :, :], idx[:, :, :]).then_inc(idx_ready, 1)

            def b_wsum(n):
                dve.wait_ge(w_ready, at(1, n, 0))
                V.tensor_reduce(w_sum[:, 0, :], w[:, :, :], AX.X, ALU.add).then_inc(w_sum_ready, 1)
                dve.wait_ge(w_sum_ready, at(2, n, 0))
                V.reciprocal(w_sum[:, 1, :], w_sum[:, 0, :]).then_inc(w_sum_ready, 1)

            def b_qkv(n, j):
                fill, ep, t = B_QKV + j, j // NT, j % NT
                dve.wait_ge(b_fill, b_at(n, fill))
                if j == 0:
                    dve.wait_ge(rw_ready, at(1, n, 0))
                if ep == 0 and not (known(n) and n == 0):
                    dve.wait_ge(qkv_ready, at(NT, n - 1, t))
                for k in range(2):
                    e = 2 * ep + k
                    lo = (E if ep == 0 else 0) + k * QKV
                    src = bank_b(fill)[:, lo:lo + QKV]
                    if ep == 0:
                        V.tensor_scalar(acc[:, t, k, :], src, rw[:, t, e:e + 1], None, ALU.mult).then_inc(b_evac, 1)
                    else:
                        dve.wait_ge(b_evac, b_read(n, fill - NT) - 1 + k)
                        V.scalar_tensor_tensor(acc[:, t, k, :], src, rw[:, t, e:e + 1], acc[:, t, k, :],
                                               ALU.mult, ALU.add).then_inc(b_evac, 1)

            def c_part(n, fill, which, pair, src):
                dve.wait_ge(c_hi, at(3, n, which))
                V.tensor_tensor(pair[1], src, pair[0].bitcast(F32), ALU.subtract).then_inc(c_evac, 1)

            def c_qk(n):
                c_part(n, C_QK, 1, flat(qkT, slice(None), slice(None), slice(None)), bank_c(C_QK)[0:D, :])

            def c_s(n):
                dve.wait_ge(c_fill, c_at(n, C_S))
                apart(dve)
                for t in range(NT):
                    keys = slice(t * P, t * P + (t + 1) * P)
                    V.tensor_tensor_reduce(out=p2[:, keys], in0=bank_c(C_S)[:, keys], in1=causal[:, T - (t + 1) * P:T],
                                           scale=-SCALE, scalar=BIG, op0=ALU.add, op1=ALU.min,
                                           accum_out=m2[:, t:t + 1]).then_inc(c_evac, 1)

            def c_pT(n):
                c_part(n, C_PT, 2, flat(p2T, slice(None), slice(None), slice(None)), bank_c(C_PT)[:, 0:3 * P])

            def c_p(n):
                dve.wait_ge(p2_exp, at(NT, n, NT - 1))
                V.reciprocal(p2_sum[:, 1, :], p2_sum[:, 0, :]).then_inc(p2_sum_ready, 1)
                dve.wait_ge(p2_sum_ready, at(1, n, 0))
                for t in range(NT):
                    keys = slice(t * P, t * P + (t + 1) * P)
                    V.tensor_scalar(p2[:, keys], p2[:, keys], p2_sum[:, 1, t:t + 1], None, ALU.mult).then_inc(p2_ready, 1)

            def c_rT(n):
                rows = slice(RG, 2 * RG)
                dve.wait_ge(c_hi, at(3, n, 0))
                V.tensor_tensor(rwT[rows, :], bank_c(C_RT)[rows, 0:T], rwT.bitcast(F32)[rows, :],
                                ALU.subtract).then_inc(c_evac, 1)

            def c_mix(n, j):
                dve.wait_ge(c_fill, c_at(n, C_RW + j))
                dve.wait_ge(c_evac, c_read(n, C_PV))
                if j == 3 and not (known(n) and n == 0):
                    dve.wait_ge(y_out, 16 * n)
                V.tensor_tensor(mix[:, 2 * j:2 * j + 2, :], bank_c(C_RW + j)[:, :].rearrange("p (a b) -> p a b", a=2),
                                aT2[:, :].unsqueeze(1).to_broadcast([P, 2, T]), ALU.mult).then_inc(c_evac, 1)

            def c_y(n):
                dve.wait_ge(c_fill, c_at(n, C_Y))
                dve.wait_ge(x2_moved, at(1, n, 0))
                V.tensor_tensor(y[:, :, :].rearrange("p a b -> p (a b)"), bank_c(C_Y)[:, :],
                                x2b[:, :, :].rearrange("p a b -> p (a b)"), ALU.add).then_inc(c_evac, 1)

            def step(i):
                ahead, now, before, before2 = i + 1, i, i - 1, i - 2

                def do(n, fn, *k):
                    if on(n):
                        fn(n, *k)

                do(before2, b_qkv, 9)
                do(before, a_pT, 2)
                do(before, a_pT, 3)
                do(before2, b_qkv, 10)
                do(before2, b_qkv, 11)
                do(now, ln1_a)
                do(before, a_pv, 1)
                do(now, ln1_b)
                do(before2, b_qkv, 12)
                do(before2, b_qkv, 13)
                do(before, a_y)
                do(now, a_cT)
                do(before, ln2_a)
                do(before2, b_qkv, 14)
                do(before2, b_qkv, 15)
                do(before, ln2_b)
                do(now, a_xT)
                do(before, b_xT, 0)
                do(before2, c_rT)
                do(before2, c_qk)
                do(before, b_xT, 1)
                do(now, a_v)
                do(now, a_kT)
                do(before2, c_s)
                do(before, b_route)
                do(before2, c_p)
                do(now, a_q, 0)
                do(now, a_q, 1)
                do(before2, c_pT)
                do(now, a_s, 0)
                do(before, b_wsum)
                do(before2, c_mix, 0)
                do(before, b_qkv, 0)
                do(before2, c_mix, 1)
                do(before, b_qkv, 1)
                do(before, b_qkv, 2)
                do(before2, c_mix, 2)
                do(before2, c_mix, 3)
                do(before, b_qkv, 3)
                do(now, a_s, 1)
                do(before, b_qkv, 4)
                do(now, a_psum, 0)
                do(before, b_qkv, 5)
                do(now, a_s, 2)
                do(before, b_qkv, 6)
                do(now, a_s, 3)
                do(before, b_qkv, 7)
                do(now, a_pT, 0)
                do(now, a_pT, 1)
                do(now, a_psum, 1)
                do(before, b_qkv, 8)
                do(before2, c_y)
                do(now, a_pv, 0)

            for i in range(-1, 3):
                step(i)
            with dve.Fori(3, B - 2) as i:
                step(i)
            for i in range(B - 2, B + 2):
                step(i)

        @block.gpsimd
        def _(pool):
            G = nc.gpsimd
            CHAIN = 10

            G.memset(ident[:, :], 0.0).then_inc(pool_step, 1)
            G.memset(causal[:, :], 0.0).then_inc(pool_step, 1)
            G.memset(rw_c[:, :, :], 0.0).then_inc(pool_step, 1)
            G.memset(sel_raw[:, :], 0.0).then_inc(pool_step, 1)
            G.iota(iota_i[:, :], pattern=[[1, E]], base=0, channel_multiplier=0).then_inc(pool_step, 1)
            pool.wait_ge(pool_step, 5)
            G.affine_select(out=ident[:, :], in_=ident[:, :], compare_op=ALU.not_equal, fill=1.0, base=0,
                            pattern=[[-1, P]], channel_multiplier=1).then_inc(consts, 1)
            G.affine_select(out=causal[:, :], in_=causal[:, :], compare_op=ALU.is_ge, fill=MASKED, base=P,
                            pattern=[[-1, T]], channel_multiplier=1).then_inc(pool_step, 1)
            sel_4d = sel_raw.rearrange("p (a b d) -> p a b d", a=EP, b=2)
            for k in range(2):
                if k:
                    pool.wait_ge(pool_step, 7)
                G.affine_select(out=sel_4d, in_=sel_4d, compare_op=ALU.not_equal, fill=1.0, base=-k * RG,
                                pattern=[[-2, EP], [-1, 2], [0, D]], channel_multiplier=1).then_inc(pool_step, 1)
            G.tensor_copy(iota[:, :], iota_i[:, :]).then_inc(pool_step, 1)
            pool.wait_ge(pool_step, 9)
            pool.wait_ge(sim_norm, 2)
            pool.wait_ge(consts, 4)
            G.tensor_tensor(sim_n[:, :], sim_n[:, :], expo[:, NT:NT + 1].to_broadcast([P, E]), ALU.pow).then_inc(sim_norm, 1)
            START = 9

            def chain(n, which):
                return CHAIN * n + which + 1 + START

            def power(n, k):
                pool.wait_ge(ln_var[k], at(k + 1, n, k))
                m = (k + 1) * NT
                src = pow_in[k][:, :, :].rearrange("p a b -> p (a b)")[:, 0:m]
                dst = pow_out[k][:, :, :].rearrange("p a b -> p (a b)")[:, 0:m]
                if not (known(n) and n == 0):
                    pool.wait_ge(ln_done[k], at(NT, n - 1, NT - 1))
                    if k == 1:
                        pool.wait_ge(rn_step, at(3, n - 1, 0))
                G.tensor_tensor(dst, src, expo[:, 0:m], ALU.pow).then_inc(ln_pow[k], 1)

            def a_xb(n):
                pool.wait_ge(x_in, 16 * (n + 1))
                if known(n) and n == 0:
                    pool.wait_ge(small_in, 48)
                else:
                    pool.wait_ge(a_evac, a_read(n - 1, A_Y))
                G.tensor_tensor(xb[:, :, :], xt[:, :, :], bo_all[:, :].unsqueeze(1).to_broadcast([P, NT, C]),
                                ALU.add).then_inc(xb_ready, 1)

            def x2_move(n):
                pool.wait_ge(a_evac, a_read(n, A_Y))
                if not (known(n) and n == 0):
                    pool.wait_ge(c_evac, c_read(n - 1, C_Y))
                apart(pool)
                G.tensor_copy(x2b[:, :, :], x2a[:, :, :]).then_inc(x2_moved, 1)

            def b_route_1(n):
                pool.wait_ge(idx_ready, at(3, n, 2))
                apart(pool)
                G.tensor_scalar(z_top[:, :], top[:, :, 0], 0.0, None, ALU.max).then_inc(pool_step, 1)
                G.tensor_scalar(idle[:, :], top[:, :, 0], 0.0, None, ALU.is_le).then_inc(pool_step, 1)
                G.tensor_scalar(g[:, :, :], z[:, :, :], 0.0, None, ALU.max).then_inc(pool_step, 1)
                G.tensor_scalar(act_on[:, :, :], z[:, :, :], 0.0, None, ALU.is_gt).then_inc(pool_step, 1)
                pool.wait_ge(pool_step, chain(n, 3))
                G.tensor_tensor(g[:, :, :], g[:, :, :], z_top[:, :].unsqueeze(2).to_broadcast([P, NT, E]),
                                ALU.subtract).then_inc(g_ready, 1)

            def b_route_2(n):
                for t in range(NT):
                    G.tensor_scalar(first[:, t, :], iota[:, :], idxf[:, t, 0:1], idle[:, t:t + 1],
                                    ALU.is_equal, ALU.mult).then_inc(pool_step, 1)
                    G.tensor_scalar(second[:, t, :], iota[:, :], idxf[:, t, 1:2], idle[:, t:t + 1],
                                    ALU.is_equal, ALU.mult).then_inc(pool_step, 1)
                pool.wait_ge(pool_step, chain(n, 7))
                G.tensor_tensor(first[:, :, :], first[:, :, :], second[:, :, :], ALU.add).then_inc(pool_step, 1)
                pool.wait_ge(pool_step, chain(n, 8))
                G.tensor_tensor(act_on[:, :, :], act_on[:, :, :], first[:, :, :], ALU.add).then_inc(pool_step, 1)

            def b_w(n):
                pool.wait_ge(pool_step, chain(n, 9))
                pool.wait_ge(e_ready, at(1, n, 0))
                G.tensor_tensor(w[:, :, :], w[:, :, :], act_on[:, :, :], ALU.mult).then_inc(w_ready, 1)

            def b_rw(n):
                pool.wait_ge(w_sum_ready, at(2, n, 1))
                if not (known(n) and n == 0):
                    pool.wait_ge(rw_c_ready, at(2, n - 1, 1))
                G.tensor_tensor(rw[:, :, :], w[:, :, :], w_sum[:, 1, :].unsqueeze(2).to_broadcast([P, NT, E]),
                                ALU.mult).then_inc(rw_ready, 1)

            def b_rw_copy(n):
                pool.wait_ge(rw_ready, at(1, n, 0))
                if not (known(n) and n == 0):
                    pool.wait_ge(c_fill, c_at(n - 1, C_RT))
                apart(pool)
                for k in range(2):
                    G.tensor_copy(rw_c[:, :, k * RG:k * RG + E], rw[:, :, :]).then_inc(rw_c_ready, 1)

            def b_sum(n, t):
                pool.wait_ge(b_evac, b_read(n, B_QKV + NT * (EP - 1) + t))
                if not (known(n) and n == 0):
                    pool.wait_ge(v2_ready, at(2, n - 1, 1))
                    pool.wait_ge(c_fill, c_at(n - 1, C_QK))
                G.tensor_tensor(qkv[:, t, :], acc[:, t, 0, :], acc[:, t, 1, :], ALU.add).then_inc(qkv_ready, 1)

            def c_v(n):
                pool.wait_ge(qkv_ready, at(NT, n, NT - 1))
                if not (known(n) and n == 0):
                    pool.wait_ge(c_fill, c_at(n - 1, C_PV))
                apart(pool)
                v_in = qkv[:, :, 2 * D:QKV].unsqueeze(2).to_broadcast([P, NT, 2, D])
                G.tensor_copy(v2[0][:, :, :, :], v_in).then_inc(v2_ready, 1)
                pool.wait_ge(v2_ready, at(2, n, 0))
                G.tensor_tensor(v2[1][:, :, :, :], v_in, v2[0].bitcast(F32)[:, :, :, :], ALU.subtract).then_inc(v2_ready, 1)

            def a_p(n, half):
                pool.wait_ge(p_sum_ready, at(4, n, 2 * half + 1))
                part = probs[:, :, half * HB:(half + 1) * HB, :]
                G.tensor_tensor(part, part, p_sum[:, half, 1, :, :].unsqueeze(3).to_broadcast([P, NT, HB, NC]),
                                ALU.mult).then_inc(p_ready, 1)

            def c_mix(n, j):
                pool.wait_ge(mix_hi, at(4, n, j))
                G.tensor_tensor(mixs[1][:, 2 * j:2 * j + 2, :], mix[:, 2 * j:2 * j + 2, :],
                                mixs[0].bitcast(F32)[:, 2 * j:2 * j + 2, :], ALU.subtract).then_inc(mix_lo, 1)

            def step(i):
                ahead, now, before, before2 = i + 1, i, i - 1, i - 2

                def do(n, fn, *k):
                    if on(n):
                        fn(n, *k)

                do(now, power, 0)
                do(before2, x2_move)
                do(before, power, 1)
                do(before2, b_sum, 0)
                do(before2, b_rw_copy)
                do(before2, b_sum, 1)
                do(before2, c_v)
                do(before, b_route_1)
                do(before, b_route_2)
                do(before, b_w)
                do(before, b_rw)
                do(before2, c_mix, 0)
                do(before2, c_mix, 1)
                do(before2, c_mix, 2)
                do(before2, c_mix, 3)
                do(now, a_xb)
                do(now, a_p, 0)
                do(now, a_p, 1)

            for i in range(-1, 3):
                step(i)
            with pool.Fori(3, B - 2) as i:
                step(i)
            for i in range(B - 2, B + 2):
                step(i)


_INS = ['x', 'ctx_768', 'L0_xattn_Wq', 'L0_xattn_Wk', 'L0_xattn_Wv', 'L0_xattn_Wo', 'L0_xattn_bo', 'L0_ffn_sim_matrix',
        'L0_ffn_gates', 'L0_ffn_q_proj', 'L0_ffn_k_proj', 'L0_ffn_v_proj', 'L0_ffn_o_proj']


def kernel(**inputs):
    import numpy as _np
    import concourse.bacc as _bacc
    from concourse import mybir as _mybir
    from concourse.bass_utils import run_bass_kernel_spmd as _run

    nc = _bacc.Bacc("TRN2", target_bir_lowering=False, num_devices=1)
    arrays, args = {}, []
    for name in _INS:
        a = _np.ascontiguousarray(inputs[name])
        arrays[f"in_{name}_dram"] = a
        args.append(nc.dram_tensor(f"in_{name}_dram", a.shape, _mybir.dt.from_np(a.dtype), kind="ExternalInput").ap())
    shape = inputs['x'].shape
    args.append(nc.dram_tensor("out_0_dram", shape, _mybir.dt.float32, kind="ExternalOutput").ap())
    xattn_moe_kernel(nc, *args)
    r = _run(nc, [arrays], core_ids=[0])
    return r.results[0]["out_0_dram"]
```

```python
import concourse.bass as bass
from concourse import mybir
from concourse.alu_op_type import AluOpType as ALU
from contextlib import ExitStack

F32 = mybir.dt.float32
F32R = mybir.dt.float32r
U32 = mybir.dt.uint32
ACT = mybir.ActivationFunctionType
AX = mybir.AxisListType


def xattn_moe_kernel(nc, x, ctx_in, Wq, Wk, Wv, Wo, bo, sim_matrix, gates, q_proj, k_proj, v_proj, o_proj, out, rw_dram):
    B, T, C = x.shape
    NC, DC = ctx_in.shape[1:]
    P = 128
    NT = T // P
    CC = C // P
    INNER = Wq.shape[1]
    D = 64
    H = INNER // D
    HC = INNER // P
    NCE = NC + NC % 2
    E = sim_matrix.shape[1]
    QKV = 3 * D
    EP = E // 2
    assert DC == P + D
    EPS = 1e-5
    TINY = 1e-12
    SCALE = D ** -0.5
    MASKED = -1e30
    BIG = 3e38

    A_CT, A_K, A_XT, A_V, A_KT, A_Q, A_S, A_Y = 0, 1, 2, 3, 4, 5, 7, 17
    A_PT, A_PV = (11, 12, 14, 15), (13, 16)
    A_FILLS, A_BANKS = 18, 3
    B_XT, B_QKV = 0, 2
    B_FILLS, B_BANKS = B_QKV + NT * EP, 3
    C_RT, C_QK, C_S, C_PT, C_PV, C_Y = 0, 1, 2, 3, 4, 5
    C_FILLS, C_BANKS = 6, 2
    assert A_FILLS % A_BANKS == 0 and B_FILLS % B_BANKS == 0 and C_FILLS % C_BANKS == 0
    HB = H // 2

    def a_at(n, fill):
        return A_FILLS * n + fill + 1

    def b_at(n, fill):
        return B_FILLS * n + fill + 1

    def c_at(n, fill):
        return C_FILLS * n + fill + 1

    def a_read(n, fill):
        assert fill % A_FILLS != A_K
        return (A_FILLS - 1) * n + fill + (1 if fill < A_K else 0)

    def b_read(n, fill):
        return (B_QKV + 2 * NT * EP) * n + (fill + 1 if fill < B_QKV else 2 * fill)

    C_READ = {C_QK: 0, C_S: 2, C_PT: 3, C_Y: 4}

    def c_read(n, fill):
        return 5 * n + C_READ[fill] + 1

    A_HI = {fill: k for k, fill in enumerate((A_CT, A_XT, A_V, A_KT, A_Q, A_Q + 1, A_PT[0], A_PT[1], A_PV[0],
                                              A_PT[2], A_PT[3], A_PV[1]))}

    def a_hi_at(n, fill):
        return len(A_HI) * n + A_HI[fill] + 1

    def at(per_batch, n, which):
        return per_batch * n + which + 1

    def known(n):
        return isinstance(n, int)

    def on(n):
        return not known(n) or 0 <= n < B

    es = ExitStack()
    with es:
        def sb(name, shape, dt=F32):
            return es.enter_context(nc.sbuf_tensor(name, shape, dt))

        def split(name, shape):
            return sb(name + "_hi", shape, F32R), sb(name + "_lo", shape, F32R)

        def sem(name):
            return es.enter_context(nc.semaphore(name))

        wq = split("wq", [P, CC, INNER])
        wk = sb("wk_hi", [P, 2, INNER], F32R), sb("wk_lo", [P, INNER], F32R)
        wv = sb("wv_hi", [P, 2, INNER], F32R), sb("wv_lo", [P, INNER], F32R)
        wo = split("wo", [P, HC, C])
        wqkv = split("wqkv", [P, CC, E + E * QKV])
        wo2 = split("wo2", [P, EP, C])
        wsim = [t[:, :, 0:E] for t in wqkv]
        bo_all = sb("bo_all", [P, C])
        sig = sb("sig", [P, E])
        ident = sb("ident", [P, P])
        causal = sb("causal", [P, T])
        expo = sb("expo", [P, 2 * NT])
        iota = sb("iota", [P, E])
        xt = sb("xt", [P, NT, C])
        xb = sb("xb", [P, NT, C])
        xn = sb("xn", [P, NT, C])
        x2_tiles = sb("x2_tiles", [P, 2 * NT * C])
        x2a, x2n = [x2_tiles[:, k * NT * C:(k + 1) * NT * C].rearrange("p (t c) -> p t c", t=NT) for k in range(2)]
        late_tiles = sb("late_tiles", [P, NT * C + NT * QKV + P + T])
        x2b = late_tiles[:, 0:NT * C].rearrange("p (t c) -> p t c", t=NT)
        stats = [sb(f"stats{k}", [P, NT, 6]) for k in (1, 2)]
        mv = [sb(f"mv{k}", [P, NT, 2]) for k in (1, 2)]
        pow_in = [sb(f"pow_in{k}", [P, 2, NT]) for k in (1, 2)]
        pow_out = [sb(f"pow_out{k}", [P, 2, NT]) for k in (1, 2)]
        rn = sb("rn", [P, 3, NT])
        ct = sb("ct", [NC, 2 * P])
        xT = split("xT", [P, CC, T])
        cT = split("cT", [P, 2, NCE])
        qT = split("qT", [P, HC, T])
        kT = split("kT", [P, HC, 2, NCE])
        v = split("v", [NC, HC, 3, D])
        s_max = sb("s_max", [P, 2 * NT, HB])
        probs = sb("probs", [P, NT, H, NC])
        pT = split("pT", [NC, HB, T])
        p_sum = sb("p_sum", [P, 2, 2, NT, HB])
        aT = split("aT", [P, HC, T])
        x2T = split("x2T", [P, CC, T])
        rwT = sb("rwT", [E, T])
        rw_all = sb("rw_all", [P, EP, T])
        z = sb("z", [P, NT, E])
        top = sb("top", [P, NT, 8])
        idx = sb("idx", [P, NT, 8], U32)
        idxf = sb("idxf", [P, NT, 8])
        z_top = sb("z_top", [P, NT])
        idle = sb("idle", [P, NT])
        first = sb("first", [P, NT, E])
        second = sb("second", [P, NT, E])
        act_on = sb("act_on", [P, NT, E])
        g = sb("g", [P, NT, E])
        w = sb("w", [P, NT, E])
        w_sum = sb("w_sum", [P, 2, NT])
        rw = sb("rw", [P, NT, E])
        acc = sb("acc", [P, NT, 2, QKV])
        qkv = late_tiles[:, NT * C:NT * (C + QKV)].rearrange("p (t f) -> p t f", t=NT)
        qk_hi = sb("qk_hi", [P, T], F32R)
        q_stack = sb("q_stack", [P, T], F32R)
        k_stack = sb("k_stack", [P, T], F32R)
        v2 = split("v2", [P, NT, 2, D])
        m2 = sb("m2", [P, NT])
        p2 = late_tiles[:, NT * (C + QKV):]
        p2_sum = sb("p2_sum", [P, 2, NT])
        p2T = split("p2T", [P, 3, P])
        aT2 = sb("aT2", [P, T])
        mix = sb("mix", [P, EP, T])
        mixs = split("mixs", [P, EP, T])
        y = mix[:, EP - NT:EP, :]

        banks_a = [es.enter_context(nc.psum_tensor(f"bank_a{k}", [P, 512], F32)) for k in range(A_BANKS)]
        banks_b = [es.enter_context(nc.psum_tensor(f"bank_b{k}", [P, 512], F32)) for k in range(B_BANKS)]
        banks_c = [es.enter_context(nc.psum_tensor(f"bank_c{k}", [P, 512], F32)) for k in range(C_BANKS)]

        def bank_a(fill):
            return banks_a[fill % A_BANKS]

        def bank_b(fill):
            return banks_b[fill % B_BANKS]

        def bank_c(fill):
            return banks_c[fill % C_BANKS]

        a_fill, a_hi, a_evac = sem("a_fill"), sem("a_hi"), sem("a_evac")
        b_fill, b_hi, b_evac = sem("b_fill"), sem("b_hi"), sem("b_evac")
        c_fill, c_hi, c_evac = sem("c_fill"), sem("c_hi"), sem("c_evac")
        x_in, ct_in, y_out = sem("x_in"), sem("ct_in"), sem("y_out")
        ln_stats = [sem(f"ln_stats{k}") for k in (1, 2)]
        ln_var = [sem(f"ln_var{k}") for k in (1, 2)]
        ln_pow = [sem(f"ln_pow{k}") for k in (1, 2)]
        ln_done = [sem(f"ln_done{k}") for k in (1, 2)]
        rn_step = sem("rn_step")
        k_ready = sem("k_ready")
        xb_ready, x2_moved = sem("xb_ready"), sem("x2_moved")
        s_max_ready, p_exp, p_sum_ready, p_ready = sem("s_max_ready"), sem("p_exp"), sem("p_sum_ready"), sem("p_ready")
        top_ready, idx_ready = sem("top_ready"), sem("idx_ready")
        pool_step = sem("pool_step")
        g_ready, e_ready, w_ready, w_sum_ready = sem("g_ready"), sem("e_ready"), sem("w_ready"), sem("w_sum_ready")
        rw_ready, qkv_ready, v2_ready = sem("rw_ready"), sem("qkv_ready"), sem("v2_ready")
        rwT_ready, rwT_out, rw_all_in, aT2_ready = sem("rwT_ready"), sem("rwT_out"), sem("rw_all_in"), sem("aT2_ready")
        p2_exp, p2_sum_ready, p2_ready = sem("p2_exp"), sem("p2_sum_ready"), sem("p2_ready")
        mix_ready, mix_hi, mix_lo = sem("mix_ready"), sem("mix_hi"), sem("mix_lo")
        consts, wt_in, wt_hi, wt_ready = sem("consts"), [sem(f"wt_in{k}") for k in range(4)], sem("wt_hi"), sem("wt_ready")
        small_in, sig_step, sim_step, sim_norm = sem("small_in"), sem("sig_step"), sem("sim_step"), sem("sim_norm")
        pad_done = sem("pad_done")
        passed = sem("passed")

        setup = acc[:, :, :, :].rearrange("p a b c -> p (a b c)")
        ones = setup[:, 0:P]
        sim_raw, sim_sq = [setup[:, P + k * CC * E:P + (k + 1) * CC * E].rearrange("p (a b) -> p a b", a=CC) for k in range(2)]
        sim_n, half_e, iota_i = [setup[:, P + (2 * CC + k) * E:P + (2 * CC + k + 1) * E] for k in range(3)]
        iota_i = iota_i.bitcast(mybir.dt.int32)
        k_rows = probs[:, :, :, :].rearrange("p a b c -> p (a b c)")[0:NC, 0:INNER]
        def apart(eng):
            eng.sem_inc(passed, 1)

        SP_COLS = EP * T // 2
        stage = [*[mix[:, k * EP // 2:(k + 1) * EP // 2, :].rearrange("p a b -> p (a b)") for k in range(2)],
                 x2_tiles[:, 0:SP_COLS], late_tiles[:, 0:SP_COLS]]
        SLOTS = len(stage)
        E4 = E // 4

        def proj_piece(cc, quarter):
            e0, e1 = quarter * E4, (quarter + 1) * E4
            loads = [(lambda s, k=k: s[:, 0:E4 * QKV].rearrange("p (e f) -> p e f", f=QKV)[:, :, k * D:(k + 1) * D],
                      w_[e0:e1, cc * P:(cc + 1) * P, :].rearrange("e c d -> c e d"))
                     for k, w_ in enumerate((q_proj, k_proj, v_proj))]
            hi, lo = [t[:, cc, E + e0 * QKV:E + e1 * QKV] for t in wqkv]
            return loads, hi, [(lo, hi, slice(0, P), slice(0, E4 * QKV))]

        def chunked_piece(dst, src, n):
            cols = n * src.shape[2]
            hi, lo = [t.rearrange("p a b -> p (a b)") for t in dst]
            return ([(lambda s: s[:, 0:cols].rearrange("p (a b) -> p a b", a=n), src)], hi,
                    [(lo, hi, slice(0, P), slice(0, cols))])

        def context_piece(dst, src):
            hi, lo = dst
            return ([(lambda s: s[:, 0:INNER], src[0:P, :]), (lambda s: s[0:D, INNER:2 * INNER], src[P:DC, :]),
                     (lambda s: s[D:P, INNER:2 * INNER], src[P:DC, :])], hi[:, :, :].rearrange("p a b -> p (a b)"),
                    [(lo[:, :], hi[:, 0, :], slice(0, P), slice(0, INNER)),
                     (hi[D:P, 1, :], hi[D:P, 1, :], slice(D, P), slice(INNER, 2 * INNER))])

        wo2_rows = o_proj.rearrange("(a e) d b -> (e d) a b", e=2)
        PIECES = [
            context_piece(wk, Wk),
            context_piece(wv, Wv),
            chunked_piece([t[:, :, :] for t in wq], Wq.rearrange("(a p) b -> p a b", p=P), CC),
            chunked_piece([t[:, :, :] for t in wo], Wo.rearrange("(a p) b -> p a b", p=P), HC),
            *[proj_piece(cc, quarter) for quarter in range(4) for cc in range(CC)],
            *[chunked_piece([t[:, k * EP // 2:(k + 1) * EP // 2, :] for t in wo2],
                            wo2_rows[:, k * EP // 2:(k + 1) * EP // 2, :], EP // 2) for k in range(2)],
        ]
        W_K, W_V, W_Q, W_O, W_QKV, W_O2 = 0, 1, 2, 3, (5, 7, 9, 11), 13
        assert len(PIECES) == W_O2 + 1 and all(piece[1].shape[1] <= SP_COLS for piece in PIECES)

        def loads_before(piece):
            return sum(len(PIECES[k][0]) for k in range(piece % SLOTS, piece + 1, SLOTS))

        EARLY = 2
        LATER = {"a_xT 0": (W_Q,), "a_v 0": (W_O,), "a_q 0 0": (4,), "a_q 0 1": (5,), "a_s 0 0": (6,), "a_s 0 1": (7,),
                 "a_pT 0 1": (8, 9), "a_pv 0 0": (10, 11), "a_pv 0 1": (12, 13)}
        assert sorted(sum(LATER.values(), ())) == list(range(EARLY, len(PIECES)))

        def later(split_piece, name, n, *k):
            if known(n) and n == 0:
                for piece in LATER.get(" ".join([name, "0", *map(str, k)]), ()):
                    split_piece(piece)

        block = es.enter_context(nc.Block())

        @block.sync
        def _(sp):
            def load_x(n):
                if not (known(n) and n == 0):
                    sp.wait_ge(xb_ready, at(1, n - 1, 0))
                    sp.wait_ge(ln_done[0], at(NT, n - 1, NT - 1))
                sp.dma_start(xt[:, :, :], x[n, :, :].rearrange("(t p) c -> p t c", p=P)).then_inc(x_in, 16)

            def load_ctx(n):
                if not (known(n) and n == 0):
                    sp.wait_ge(a_fill, a_at(n - 1, A_CT))
                sp.dma_start(ct[:, 0:DC], ctx_in[n, :, :]).then_inc(ct_in, 16)
                sp.dma_start(ct[:, DC:2 * P], ctx_in[n, :, P:DC]).then_inc(ct_in, 16)

            def store(n):
                sp.wait_ge(c_evac, c_read(n, C_Y))
                sp.dma_start(out[n, :, :].rearrange("(t p) c -> p t c", p=P), y[:, :, :]).then_inc(y_out, 16)

            def spread_rw(n):
                sp.wait_ge(rwT_ready, at(1, n, 0))
                sp.dma_start(rw_dram[:, :], rwT[:, :]).then_inc(rwT_out, 16)
                sp.wait_ge(rwT_out, 16 * (n + 1))
                if not (known(n) and n == 0):
                    sp.wait_ge(mix_ready, at(4, n - 1, 3))
                for k in range(2):
                    sp.dma_start(rw_all[k * D:(k + 1) * D, :, :],
                                 rw_dram[:, :].rearrange("(a k) t -> k a t", k=2)[k].partition_broadcast(D)).then_inc(rw_all_in, 16)

            load_x(0)
            load_ctx(0)
            sp.dma_start(sim_raw[:, :, :], sim_matrix.rearrange("(a p) e -> p a e", p=P)).then_inc(small_in, 16)
            sp.dma_start(sig[:, :], gates.partition_broadcast(P)).then_inc(small_in, 16)
            sp.dma_start(bo_all[:, :], bo.partition_broadcast(P)).then_inc(small_in, 16)

            def load_weights(pieces):
                for k in pieces:
                    if k >= SLOTS:
                        sp.wait_ge(wt_ready, k - SLOTS + 1)
                    for view, src in PIECES[k][0]:
                        sp.dma_start(view(stage[k % SLOTS]), src).then_inc(wt_in[k % SLOTS], 16)

            load_weights(range(SLOTS + 3))

            def step(i):
                if on(i - 2):
                    store(i - 2)
                if on(i - 1):
                    spread_rw(i - 1)
                if on(i + 2):
                    load_ctx(i + 2)
                if on(i + 2):
                    load_x(i + 2)

            step(-1)
            load_weights(range(SLOTS + 3, len(PIECES)))
            for i in range(3):
                step(i)
            with sp.Fori(3, B - 2) as i:
                step(i)
            for i in range(B - 2, B + 2):
                step(i)
            sp.wait_ge(y_out, 16 * B)

        @block.tensor
        def _(pe):
            def product(dst, lhs, rhs, start=True, stop=True):
                nc.tensor.matmul(dst, lhs[1], rhs[0], start=start, stop=False)
                nc.tensor.matmul(dst, lhs[0], rhs[1], start=False, stop=False)
                return nc.tensor.matmul(dst, lhs[0], rhs[0], start=False, stop=stop)

            def part(pair, *at_):
                return [t[at_] for t in pair]

            def ring_a(n, fill):
                if fill - A_BANKS == A_K:
                    pe.wait_ge(k_ready, at(1, n, 0))
                elif fill >= A_BANKS:
                    pe.wait_ge(a_evac, a_read(n, fill - A_BANKS))
                elif not (known(n) and n == 0):
                    pe.wait_ge(a_evac, a_read(n - 1, fill - A_BANKS + A_FILLS))

            def ring_b(n, fill):
                if not (known(n) and n == 0 and fill < B_BANKS):
                    if fill >= B_BANKS:
                        pe.wait_ge(b_evac, b_read(n, fill - B_BANKS))
                    else:
                        pe.wait_ge(b_evac, b_read(n - 1, fill - B_BANKS + B_FILLS))

            def ring_c(n, fill):
                before, m = (fill - C_BANKS, n) if fill >= C_BANKS else (fill - C_BANKS + C_FILLS, n - 1)
                if not (known(m) and m < 0):
                    if before == C_RT:
                        pe.wait_ge(rwT_ready, at(1, m, 0))
                    elif before == C_PV:
                        pe.wait_ge(aT2_ready, at(1, m, 0))
                    else:
                        pe.wait_ge(c_evac, c_read(m, before))

            def weights(n, piece):
                if known(n) and n == 0:
                    pe.wait_ge(wt_ready, piece + 1)

            def a_xT(n):
                ring_a(n, A_XT)
                pe.wait_ge(ln_done[0], at(NT, n, NT - 1))
                for cc in range(CC):
                    for t in range(NT):
                        last = nc.tensor.transpose(bank_a(A_XT)[:, cc * T + t * P:cc * T + (t + 1) * P],
                                                   xn[:, t, cc * P:(cc + 1) * P], ident[:, :])
                last.then_inc(a_fill, 1)

            def a_cT(n):
                ring_a(n, A_CT)
                pe.wait_ge(ct_in, 32 * (n + 1))
                for k in range(2):
                    last = nc.tensor.transpose(bank_a(A_CT)[:, k * P:k * P + NC], ct[:, k * P:(k + 1) * P],
                                               ident[0:NC, 0:NC])
                last.then_inc(a_fill, 1)

            def a_q(n, j):
                fill = A_Q + j
                ring_a(n, fill)
                weights(n, W_Q)
                pe.wait_ge(a_evac, a_read(n, A_XT))
                for k in range(2):
                    hc = 2 * j + k
                    for cc in range(CC):
                        last = product(bank_a(fill)[:, k * T:(k + 1) * T],
                                       part(wq, slice(None), cc, slice(hc * P, (hc + 1) * P)),
                                       part(xT, slice(None), cc, slice(None)), cc == 0, cc == CC - 1)
                last.then_inc(a_fill, 1)

            def context_product(dst, w_):
                product(dst, part(cT, slice(None), 0, slice(0, NC)), [w_[0][:, 0, :], w_[1][:, :]], True, False)
                nc.tensor.matmul(dst, cT[1][:, 1, 0:NC], w_[0][:, 1, :], start=False, stop=False)
                return nc.tensor.matmul(dst, cT[0][0:D, 1, 0:NC], w_[0][0:D, 1, :], start=False, stop=True)

            def a_k(n):
                ring_a(n, A_K)
                weights(n, W_K)
                pe.wait_ge(a_evac, a_read(n, A_CT))
                context_product(bank_a(A_K)[0:NC, :], wk).then_inc(a_fill, 1)

            def a_v(n):
                ring_a(n, A_V)
                weights(n, W_V)
                context_product(bank_a(A_V)[0:NC, :], wv).then_inc(a_fill, 1)

            def a_kT(n):
                ring_a(n, A_KT)
                pe.wait_ge(k_ready, at(1, n, 0))
                for hc in range(HC):
                    last = nc.tensor.transpose(bank_a(A_KT)[:, hc * NCE:hc * NCE + NC], k_rows[:, hc * P:(hc + 1) * P],
                                               ident[0:NC, 0:NC])
                last.then_inc(a_fill, 1)

            def a_s(n, j):
                fill, half, t = A_S + j, j // 2, j % 2
                ring_a(n, fill)
                if known(n) and n == 0:
                    pe.wait_ge(pad_done, 4)
                pe.wait_ge(a_evac, a_read(n, A_Q + half))
                for k in range(2):
                    hc = 2 * half + k
                    last = product(bank_a(fill)[:, k * 2 * NCE:(k + 1) * 2 * NCE],
                                   part(qT, slice(None), hc, slice(t * P, (t + 1) * P)),
                                   [w_[:, hc, :, :].rearrange("p a b -> p (a b)") for w_ in kT])
                last.then_inc(a_fill, 1)

            def a_pT(n, j):
                fill, half, t = A_PT[j], j // 2, j % 2
                ring_a(n, fill)
                pe.wait_ge(p_ready, at(2, n, half))
                for k in range(HB):
                    last = nc.tensor.transpose(bank_a(fill)[0:NC, k * P:(k + 1) * P], probs[:, t, half * HB + k, :], ident[:, :])
                last.then_inc(a_fill, 1)

            def a_pv(n, half):
                fill = A_PV[half]
                ring_a(n, fill)
                pe.wait_ge(a_evac, a_read(n, A_PT[2 * half + 1]))
                for k in range(2):
                    hc = 2 * half + k
                    for odd in range(2):
                        last = product(bank_a(fill)[:, k * T:(k + 1) * T],
                                       [w_[:, hc, odd:odd + 2, :].rearrange("p a b -> p (a b)") for w_ in v],
                                       part(pT, slice(None), 2 * k + odd, slice(None)), odd == 0, odd == 1)
                last.then_inc(a_fill, 1)

            def a_y(n):
                ring_a(n, A_Y)
                weights(n, W_O)
                pe.wait_ge(a_evac, a_read(n, A_PV[1]))
                for t in range(NT):
                    for hc in range(HC):
                        last = product(bank_a(A_Y)[:, t * C:(t + 1) * C], part(aT, slice(None), hc, slice(t * P, (t + 1) * P)),
                                       part(wo, slice(None), hc, slice(None)), hc == 0, hc == HC - 1)
                last.then_inc(a_fill, 1)

            def b_xT(n, t):
                ring_b(n, B_XT + t)
                pe.wait_ge(ln_done[1], at(NT, n, NT - 1))
                for cc in range(CC):
                    last = nc.tensor.transpose(bank_b(B_XT + t)[:, cc * P:(cc + 1) * P],
                                               x2n[:, t, cc * P:(cc + 1) * P], ident[:, :])
                last.then_inc(b_fill, 1)

            def b_qkv(n, j):
                fill, ep, t = B_QKV + j, j // NT, j % NT
                ring_b(n, fill)
                weights(n, W_QKV[ep * 2 // E4])
                if ep == 0:
                    if known(n) and n == 0:
                        pe.wait_ge(sim_step, 5)
                    pe.wait_ge(b_evac, b_read(n, B_XT + t))
                lo = 0 if ep == 0 else E + 2 * ep * QKV
                cols = slice(lo, E + 2 * (ep + 1) * QKV)
                for cc in range(CC):
                    last = product(bank_b(fill)[:, 0:cols.stop - lo], part(x2T, slice(None), cc, slice(t * P, (t + 1) * P)),
                                   part(wqkv, slice(None), cc, cols), cc == 0, cc == CC - 1)
                last.then_inc(b_fill, 1)

            def c_qk(n):
                ring_c(n, C_QK)
                pe.wait_ge(qkv_ready, at(NT, n, NT - 1))
                for t in range(NT):
                    last = nc.tensor.transpose(bank_c(C_QK)[:, t * P:(t + 1) * P], qkv[:, t, 0:2 * D], ident[:, :])
                last.then_inc(c_fill, 1)

            def c_s(n):
                ring_c(n, C_S)
                pe.wait_ge(c_evac, c_read(n, C_QK))
                for t in range(NT):
                    keys, dst = (t + 1) * P, bank_c(C_S)[:, t * P:t * P + (t + 1) * P]
                    nc.tensor.matmul(dst, q_stack[:, t * P:(t + 1) * P], k_stack[:, 0:keys], start=True, stop=False)
                    last = nc.tensor.matmul(dst, qk_hi[0:D, t * P:(t + 1) * P], k_stack[0:D, 0:keys], start=False, stop=True)
                last.then_inc(c_fill, 1)

            def c_pT(n):
                ring_c(n, C_PT)
                pe.wait_ge(p2_ready, at(NT, n, NT - 1))
                for k in range(3):
                    last = nc.tensor.transpose(bank_c(C_PT)[:, k * P:(k + 1) * P], p2[:, k * P:(k + 1) * P], ident[:, :])
                last.then_inc(c_fill, 1)

            def c_rT(n):
                ring_c(n, C_RT)
                pe.wait_ge(rw_ready, at(1, n, 0))
                apart(pe)
                for t in range(NT):
                    last = nc.tensor.transpose(bank_c(C_RT)[0:E, t * P:(t + 1) * P], rw[:, t, :], ident[:, :])
                last.then_inc(c_fill, 1)

            def c_pv(n):
                ring_c(n, C_PV)
                pe.wait_ge(c_evac, c_read(n, C_PT))
                pe.wait_ge(v2_ready, at(2, n, 1))
                vs = [[w_[:, t, :, :].rearrange("p a b -> p (a b)") for w_ in v2] for t in range(NT)]
                product(bank_c(C_PV)[:, 0:T], vs[0], [w_[:, 0:2, :].rearrange("p a b -> p (a b)") for w_ in p2T], True, False)
                product(bank_c(C_PV)[:, P:T], vs[1], part(p2T, slice(None), 2, slice(None)), False, True).then_inc(c_fill, 1)

            def c_y(n, quarter):
                t, half = quarter // 2, quarter % 2
                if quarter == 0:
                    ring_c(n, C_Y)
                    weights(n, W_O2)
                for ep in range(half * EP // 2, (half + 1) * EP // 2):
                    if t == 0 and ep % 2 == 0:
                        pe.wait_ge(mix_lo, at(4, n, ep // 2))
                    last = product(bank_c(C_Y)[:, t * C:(t + 1) * C],
                                   part(mixs, slice(None), ep, slice(t * P, (t + 1) * P)),
                                   part(wo2, slice(None), ep, slice(None)), ep == 0, ep == EP - 1)
                if quarter == 3:
                    last.then_inc(c_fill, 1)

            def sim_norms():
                pe.wait_ge(consts, 4)
                pe.wait_ge(sim_step, 1)
                for cc in range(CC):
                    last = nc.tensor.matmul(bank_b(0)[:, 0:E], ones[:, :], sim_sq[:, cc, :], start=cc == 0, stop=cc == CC - 1)
                last.then_inc(sim_norm, 1)

            sim_norms()

            def step(i):
                ahead, now, before, earlier = i + 1, i, i - 1, i - 2

                def do(n, fn, *k):
                    if on(n):
                        fn(n, *k)

                do(before, b_qkv, 6)
                do(before, b_qkv, 7)
                do(earlier, c_y, 0)
                do(before, b_qkv, 8)
                do(earlier, c_y, 1)
                do(now, a_pT, 0)
                do(now, a_pT, 1)
                do(earlier, c_y, 2)
                do(earlier, c_y, 3)
                do(now, a_pv, 0)
                do(now, a_pT, 2)
                do(now, a_pT, 3)
                do(before, b_qkv, 9)
                do(before, b_qkv, 10)
                do(now, a_pv, 1)
                do(before, b_qkv, 11)
                do(before, b_qkv, 12)
                do(now, a_y)
                do(before, b_qkv, 13)
                do(ahead, a_cT)
                do(before, b_qkv, 14)
                do(before, b_qkv, 15)
                do(ahead, a_k)
                do(ahead, a_xT)
                do(before, c_rT)
                do(now, b_xT, 0)
                do(now, b_xT, 1)
                do(ahead, a_v)
                do(before, c_qk)
                do(now, b_qkv, 0)
                do(now, b_qkv, 1)
                do(ahead, a_kT)
                do(before, c_s)
                do(ahead, a_q, 0)
                do(ahead, a_q, 1)
                do(now, b_qkv, 2)
                do(ahead, a_s, 0)
                do(before, c_pT)
                do(ahead, a_s, 1)
                do(ahead, a_s, 2)
                do(ahead, a_s, 3)
                do(before, c_pv)
                do(now, b_qkv, 3)
                do(now, b_qkv, 4)
                do(now, b_qkv, 5)

            for i in range(-1, 3):
                step(i)
            with pe.Fori(3, B - 2) as i:
                step(i)
            for i in range(B - 2, B + 2):
                step(i)

        @block.scalar
        def _(act):
            copy = ACT.Copy

            act.wait_ge(small_in, 48)
            nc.scalar.activation(half_e[:, :], sig[:, :], ACT.Exp, scale=-1.0).then_inc(sig_step, 1)

            def split_weights(k):
                hi = PIECES[k][1]
                act.wait_ge(wt_in[k % SLOTS], 16 * loads_before(k))
                nc.scalar.activation(hi, stage[k % SLOTS][:, 0:hi.shape[1]], copy).then_inc(wt_hi, 1)

            for k in range(EARLY):
                split_weights(k)

            def a_part(n, fill, dst, src):
                act.wait_ge(a_fill, a_at(n, fill))
                nc.scalar.activation(dst, src, copy).then_inc(a_hi, 1)

            def a_xT(n):
                a_part(n, A_XT, xT[0][:, :, :].rearrange("p a b -> p (a b)"), bank_a(A_XT)[:, :])

            def a_cT(n):
                if known(n) and n == 0:
                    act.wait_ge(pad_done, 2)
                src = bank_a(A_CT)[:, 0:2 * P].rearrange("p (a b) -> p a b", a=2)
                act.wait_ge(a_fill, a_at(n, A_CT))
                nc.scalar.activation(cT[0][:, :, 0:NC], src[:, :, 0:NC], copy)
                nc.scalar.activation(cT[1][D:P, 1, 0:NC], src[D:P, 1, 0:NC], copy).then_inc(a_hi, 1)

            def a_q(n, j):
                a_part(n, A_Q + j, qT[0][:, 2 * j:2 * j + 2, :].rearrange("p a b -> p (a b)"), bank_a(A_Q + j)[:, :])

            def a_k(n):
                act.wait_ge(a_fill, a_at(n, A_K))
                nc.scalar.activation(k_rows, bank_a(A_K)[0:NC, :], copy).then_inc(k_ready, 1)

            def a_v(n):
                if known(n) and n == 0:
                    act.wait_ge(pad_done, 4)
                a_part(n, A_V, v[0][:, :, 0:3:2, :], bank_a(A_V)[0:NC, :].rearrange("p (a b c) -> p a b c", a=HC, b=2))

            def a_kT(n):
                act.wait_ge(a_fill, a_at(n, A_KT))
                for k in range(2):
                    rows = slice(k * D, (k + 1) * D)
                    src = bank_a(A_KT)[rows, 0:HC * NCE].rearrange("p (a b) -> p a b", a=HC)[:, :, 0:NC]
                    last = nc.scalar.activation(kT[0][rows, :, k, 0:NC], src, copy)
                last.then_inc(a_hi, 1)

            def a_exp(n, j):
                half, t = j // 2, j % 2
                act.wait_ge(a_evac, a_read(n, A_S + j))
                nc.scalar.activation(probs[:, t, half * HB:(half + 1) * HB, :], probs[:, t, half * HB:(half + 1) * HB, :],
                                     ACT.Exp, scale=SCALE).then_inc(p_exp, 1)

            def a_pT(n, j):
                t = j % 2
                a_part(n, A_PT[j], pT[0][:, :, t * P:(t + 1) * P], bank_a(A_PT[j])[0:NC, :].rearrange("p (a b) -> p a b", a=HB))

            def a_pv(n, half):
                a_part(n, A_PV[half], aT[0][:, 2 * half:2 * half + 2, :].rearrange("p a b -> p (a b)"), bank_a(A_PV[half])[:, :])

            def b_xT(n, t):
                act.wait_ge(b_fill, b_at(n, B_XT + t))
                nc.scalar.activation(x2T[0][:, :, t * P:(t + 1) * P], bank_b(B_XT + t)[:, 0:CC * P].rearrange("p (a b) -> p a b", a=CC),
                                     copy).then_inc(b_hi, 1)

            def b_exp(n):
                act.wait_ge(g_ready, at(1, n, 0))
                nc.scalar.activation(w[:, :, :], g[:, :, :], ACT.Exp).then_inc(e_ready, 1)

            def c_part(n, fill, dst, src):
                act.wait_ge(c_fill, c_at(n, fill))
                nc.scalar.activation(dst, src, copy).then_inc(c_hi, 1)

            def c_qk(n):
                src = bank_c(C_QK)[:, 0:T]
                act.wait_ge(c_fill, c_at(n, C_QK))
                nc.scalar.activation(qk_hi[:, :], src, copy)
                nc.scalar.activation(q_stack[D:P, :], src[0:D, :], copy)
                nc.scalar.activation(k_stack[0:D, :], src[D:P, :], copy).then_inc(c_hi, 1)

            def c_exp(n):
                for t in range(NT):
                    keys = slice(t * P, t * P + (t + 1) * P)
                    act.wait_ge(c_evac, c_read(n, C_S) - NT + 1 + t)
                    nc.scalar.activation(p2[:, keys], p2[:, keys], ACT.Exp, bias=m2[:, t:t + 1], scale=-1.0,
                                         accum_out=p2_sum[:, 0, t:t + 1]).then_inc(p2_exp, 1)

            def c_pT(n):
                c_part(n, C_PT, p2T[0][:, :, :].rearrange("p a b -> p (a b)"), bank_c(C_PT)[:, 0:3 * P])

            def c_rT(n):
                act.wait_ge(c_fill, c_at(n, C_RT))
                if not (known(n) and n == 0):
                    act.wait_ge(rwT_out, 16 * n)
                nc.scalar.activation(rwT[:, :], bank_c(C_RT)[0:E, 0:T], copy).then_inc(rwT_ready, 1)

            def c_pv(n):
                act.wait_ge(c_fill, c_at(n, C_PV))
                nc.scalar.activation(aT2[:, :], bank_c(C_PV)[:, 0:T], copy).then_inc(aT2_ready, 1)

            def c_mix(n, j):
                act.wait_ge(mix_ready, at(4, n, j))
                nc.scalar.activation(mixs[0][:, 2 * j:2 * j + 2, :], mix[:, 2 * j:2 * j + 2, :], copy).then_inc(mix_hi, 1)

            def step(i):
                ahead, now, before, earlier = i + 1, i, i - 1, i - 2

                def do(n, fn, *k):
                    if on(n):
                        fn(n, *k)
                        later(split_weights, fn.__name__.replace("exp", "s"), n, *k)

                do(earlier, c_mix, 3)
                do(now, a_exp, 1)
                do(now, a_exp, 2)
                do(now, a_exp, 3)
                do(now, a_pT, 0)
                do(now, a_pT, 1)
                do(now, a_pv, 0)
                do(now, a_pT, 2)
                do(now, a_pT, 3)
                do(now, a_pv, 1)
                do(ahead, a_cT)
                do(ahead, a_k)
                do(ahead, a_xT)
                do(now, b_xT, 0)
                do(before, c_rT)
                do(now, b_xT, 1)
                do(ahead, a_v)
                do(before, c_qk)
                do(ahead, a_kT)
                do(ahead, a_q, 0)
                do(before, c_exp)
                do(ahead, a_q, 1)
                do(now, b_exp)
                do(before, c_pT)
                do(before, c_pv)
                do(before, c_mix, 0)
                do(ahead, a_exp, 0)
                do(before, c_mix, 1)
                do(before, c_mix, 2)

            for i in range(-1, 3):
                step(i)
            with act.Fori(3, B - 2) as i:
                step(i)
            for i in range(B - 2, B + 2):
                step(i)

        @block.vector
        def _(dve):
            V = nc.vector

            V.memset(expo[:, 0:NT], -0.5).then_inc(consts, 1)
            V.memset(expo[:, NT:2 * NT], 0.5).then_inc(consts, 1)
            V.memset(ones[:, :], 1.0).then_inc(consts, 1)
            for k in range(2):
                V.memset(cT[k].bitcast(F32)[:, :, NC:NCE], 0.0).then_inc(pad_done, 1)
            for k in range(2):
                V.memset(v[k].bitcast(F32)[:, :, :, :], 0.0)
                V.memset(kT[k].bitcast(F32)[:, :, :, :], 0.0).then_inc(pad_done, 1)
            def split_weights(k):
                dve.wait_ge(wt_hi, k + 1)
                for lo, hi, rows, cols in PIECES[k][2]:
                    last = V.tensor_tensor(lo, stage[k % SLOTS][rows, cols], hi.bitcast(F32), ALU.subtract)
                last.then_inc(wt_ready, 1)

            def ln_a(k, n, src):
                for t in range(NT):
                    V.bn_stats(stats[k][:, t, :], src[:, t, :]).then_inc(ln_stats[k], 1)
                for t in range(NT):
                    dve.wait_ge(ln_stats[k], at(2 * NT, n, t))
                    apart(dve)
                    V.bn_aggr(mv[k][:, t, :], stats[k][:, t, :]).then_inc(ln_stats[k], 1)
                dve.wait_ge(ln_stats[k], at(2 * NT, n, 2 * NT - 1))
                if k == 0:
                    V.tensor_scalar(pow_in[k][:, 0, :], mv[k][:, :, 1], EPS, None, ALU.add).then_inc(ln_var[k], 1)
                else:
                    V.tensor_scalar(pow_in[k][:, 0, :], mv[k][:, :, 1], EPS, None, ALU.add).then_inc(ln_var[k], 1)
                    V.tensor_scalar(pow_in[k][:, 1, :], mv[k][:, :, 1], float(C), None, ALU.mult).then_inc(ln_var[k], 1)

            def ln_b(k, n, src, dst):
                dve.wait_ge(ln_pow[k], at(1, n, 0))
                for t in range(NT):
                    V.tensor_scalar(dst[:, t, :], src[:, t, :], mv[k][:, t, 0:1], pow_out[k][:, 0, t:t + 1],
                                    ALU.subtract, ALU.mult).then_inc(ln_done[k], 1)

            def ln1_a(n):
                dve.wait_ge(x_in, 16 * (n + 1))
                ln_a(0, n, xt)

            def ln1_b(n):
                if not (known(n) and n == 0):
                    dve.wait_ge(a_fill, a_at(n - 1, A_XT))
                ln_b(0, n, xt, xn)

            def ln2_a(n):
                dve.wait_ge(a_evac, a_read(n, A_Y))
                ln_a(1, n, x2a)

            def ln2_b(n):
                if not (known(n) and n == 0):
                    dve.wait_ge(b_fill, b_at(n - 1, B_XT))
                ln_b(1, n, x2a, x2n)
                V.tensor_tensor(rn[:, 0, :], pow_out[1][:, 0, :], pow_out[1][:, 1, :], ALU.mult).then_inc(rn_step, 1)
                dve.wait_ge(rn_step, at(3, n, 0))
                V.tensor_scalar(rn[:, 1, :], rn[:, 0, :], TINY, None, ALU.max).then_inc(rn_step, 1)
                dve.wait_ge(rn_step, at(3, n, 1))
                V.reciprocal(rn[:, 2, :], rn[:, 1, :]).then_inc(rn_step, 1)

            def a_part(n, fill, pair, src):
                dve.wait_ge(a_hi, a_hi_at(n, fill))
                V.tensor_tensor(pair[1], src, pair[0].bitcast(F32), ALU.subtract).then_inc(a_evac, 1)

            def flat(pair, *at_):
                return [t[at_].rearrange("p a b -> p (a b)") for t in pair]

            def a_xT(n):
                a_part(n, A_XT, flat(xT, slice(None), slice(None), slice(None)), bank_a(A_XT)[:, :])

            def a_cT(n):
                src = bank_a(A_CT)[:, 0:2 * P].rearrange("p (a b) -> p a b", a=2)
                dve.wait_ge(a_hi, a_hi_at(n, A_CT))
                for rows, k in ((slice(0, P), 0), (slice(0, D), 1)):
                    last = V.tensor_tensor(cT[1][rows, k, 0:NC], src[rows, k, 0:NC], cT[0].bitcast(F32)[rows, k, 0:NC], ALU.subtract)
                last.then_inc(a_evac, 1)

            def a_q(n, j):
                a_part(n, A_Q + j, flat(qT, slice(None), slice(2 * j, 2 * j + 2), slice(None)), bank_a(A_Q + j)[:, :])

            def a_v(n):
                a_part(n, A_V, [w_[:, :, 0:3:2, :] for w_ in v],
                       bank_a(A_V)[0:NC, :].rearrange("p (a b c) -> p a b c", a=HC, b=2))

            def a_kT(n):
                dve.wait_ge(a_hi, a_hi_at(n, A_KT))
                for k in range(2):
                    rows = slice(k * D, (k + 1) * D)
                    src = bank_a(A_KT)[rows, 0:HC * NCE].rearrange("p (a b) -> p a b", a=HC)[:, :, 0:NC]
                    last = V.tensor_tensor(kT[1][rows, :, k, 0:NC], src, kT[0].bitcast(F32)[rows, :, k, 0:NC], ALU.subtract)
                last.then_inc(a_evac, 1)

            def a_s(n, j):
                half, t = j // 2, j % 2
                src = bank_a(A_S + j)[:, 0:HB * NCE].rearrange("p (a b) -> p a b", a=HB)[:, :, 0:NC]
                dve.wait_ge(a_fill, a_at(n, A_S + j))
                V.tensor_reduce(s_max[:, j, :], src, AX.X, ALU.max).then_inc(s_max_ready, 1)
                dve.wait_ge(s_max_ready, at(2 * NT, n, j))
                V.tensor_tensor(probs[:, t, half * HB:(half + 1) * HB, :], src,
                                s_max[:, j, :].unsqueeze(2).to_broadcast([P, HB, NC]), ALU.subtract).then_inc(a_evac, 1)

            def a_psum(n, half):
                dve.wait_ge(p_exp, at(2 * NT, n, 2 * half + 1))
                V.tensor_reduce(p_sum[:, half, 0, :, :], probs[:, :, half * HB:(half + 1) * HB, :], AX.X,
                                ALU.add).then_inc(p_sum_ready, 1)
                dve.wait_ge(p_sum_ready, at(4, n, 2 * half))
                V.reciprocal(p_sum[:, half, 1, :, :], p_sum[:, half, 0, :, :]).then_inc(p_sum_ready, 1)

            def a_pT(n, j):
                t = j % 2
                a_part(n, A_PT[j], [w_[:, :, t * P:(t + 1) * P] for w_ in pT],
                       bank_a(A_PT[j])[0:NC, :].rearrange("p (a b) -> p a b", a=HB))

            def a_pv(n, half):
                a_part(n, A_PV[half], flat(aT, slice(None), slice(2 * half, 2 * half + 2), slice(None)), bank_a(A_PV[half])[:, :])

            def a_y(n):
                dve.wait_ge(a_fill, a_at(n, A_Y))
                dve.wait_ge(xb_ready, at(1, n, 0))
                if not (known(n) and n == 0):
                    dve.wait_ge(x2_moved, at(1, n - 1, 0))
                V.tensor_tensor(x2a[:, :, :].rearrange("p a b -> p (a b)"), bank_a(A_Y)[:, :],
                                xb[:, :, :].rearrange("p a b -> p (a b)"), ALU.add).then_inc(a_evac, 1)

            def b_xT(n, t):
                dve.wait_ge(b_hi, at(NT, n, t))
                V.tensor_tensor(x2T[1][:, :, t * P:(t + 1) * P], bank_b(B_XT + t)[:, 0:CC * P].rearrange("p (a b) -> p a b", a=CC),
                                x2T[0].bitcast(F32)[:, :, t * P:(t + 1) * P], ALU.subtract).then_inc(b_evac, 1)

            def b_route(n):
                dve.wait_ge(rn_step, at(3, n, 2))
                for t in range(NT):
                    dve.wait_ge(b_fill, b_at(n, B_QKV + t))
                    V.scalar_tensor_tensor(z[:, t, :], bank_b(B_QKV + t)[:, 0:E], rn[:, 2, t:t + 1], sig[:, :],
                                           ALU.mult, ALU.subtract).then_inc(top_ready, 1)
                for t in range(NT):
                    dve.wait_ge(top_ready, at(4, n, t))
                    apart(dve)
                    V.max(top[:, t, :], z[:, t, :]).then_inc(top_ready, 1)
                for t in range(NT):
                    dve.wait_ge(top_ready, at(4, n, 2 + t))
                    apart(dve)
                    V.max_index(idx[:, t, :], top[:, t, :], z[:, t, :]).then_inc(idx_ready, 1)
                dve.wait_ge(idx_ready, at(3, n, 1))
                V.tensor_copy(idxf[:, :, :], idx[:, :, :]).then_inc(idx_ready, 1)

            def b_wsum(n):
                dve.wait_ge(w_ready, at(1, n, 0))
                V.tensor_reduce(w_sum[:, 0, :], w[:, :, :], AX.X, ALU.add).then_inc(w_sum_ready, 1)
                dve.wait_ge(w_sum_ready, at(2, n, 0))
                V.reciprocal(w_sum[:, 1, :], w_sum[:, 0, :]).then_inc(w_sum_ready, 1)

            def b_qkv(n, j):
                fill, ep, t = B_QKV + j, j // NT, j % NT
                dve.wait_ge(b_fill, b_at(n, fill))
                if j == 0:
                    dve.wait_ge(rw_ready, at(1, n, 0))
                if ep == 0 and not (known(n) and n == 0):
                    dve.wait_ge(qkv_ready, at(NT, n - 1, t))
                for k in range(2):
                    e = 2 * ep + k
                    lo = (E if ep == 0 else 0) + k * QKV
                    src = bank_b(fill)[:, lo:lo + QKV]
                    if ep == 0:
                        V.tensor_scalar(acc[:, t, k, :], src, rw[:, t, e:e + 1], None, ALU.mult).then_inc(b_evac, 1)
                    else:
                        dve.wait_ge(b_evac, b_read(n, fill - NT) - 1 + k)
                        V.scalar_tensor_tensor(acc[:, t, k, :], src, rw[:, t, e:e + 1], acc[:, t, k, :],
                                               ALU.mult, ALU.add).then_inc(b_evac, 1)

            def c_part(n, fill, which, pair, src):
                dve.wait_ge(c_hi, at(2, n, which))
                V.tensor_tensor(pair[1], src, pair[0].bitcast(F32), ALU.subtract).then_inc(c_evac, 1)

            def c_qk(n):
                dve.wait_ge(c_hi, at(2, n, 0))
                for stack, rows in ((q_stack, slice(0, D)), (k_stack, slice(D, P))):
                    last = V.tensor_tensor(stack[rows, :], bank_c(C_QK)[rows, 0:T], qk_hi.bitcast(F32)[rows, :], ALU.subtract)
                last.then_inc(c_evac, 1)

            def c_s(n):
                dve.wait_ge(c_fill, c_at(n, C_S))
                apart(dve)
                for t in range(NT):
                    keys = slice(t * P, t * P + (t + 1) * P)
                    V.tensor_tensor_reduce(out=p2[:, keys], in0=bank_c(C_S)[:, keys], in1=causal[:, T - (t + 1) * P:T],
                                           scale=-SCALE, scalar=BIG, op0=ALU.add, op1=ALU.min,
                                           accum_out=m2[:, t:t + 1]).then_inc(c_evac, 1)

            def c_pT(n):
                c_part(n, C_PT, 1, flat(p2T, slice(None), slice(None), slice(None)), bank_c(C_PT)[:, 0:3 * P])

            def c_p(n):
                dve.wait_ge(p2_exp, at(NT, n, NT - 1))
                V.reciprocal(p2_sum[:, 1, :], p2_sum[:, 0, :]).then_inc(p2_sum_ready, 1)
                dve.wait_ge(p2_sum_ready, at(1, n, 0))
                for t in range(NT):
                    keys = slice(t * P, t * P + (t + 1) * P)
                    V.tensor_scalar(p2[:, keys], p2[:, keys], p2_sum[:, 1, t:t + 1], None, ALU.mult).then_inc(p2_ready, 1)

            def c_mix(n, j):
                dve.wait_ge(rw_all_in, 32 * (n + 1))
                dve.wait_ge(aT2_ready, at(1, n, 0))
                if j == 3 and not (known(n) and n == 0):
                    dve.wait_ge(y_out, 16 * n)
                V.tensor_tensor(mix[:, 2 * j:2 * j + 2, :], rw_all[:, 2 * j:2 * j + 2, :],
                                aT2[:, :].unsqueeze(1).to_broadcast([P, 2, T]), ALU.mult).then_inc(mix_ready, 1)

            def c_y(n):
                dve.wait_ge(c_fill, c_at(n, C_Y))
                dve.wait_ge(x2_moved, at(1, n, 0))
                V.tensor_tensor(y[:, :, :].rearrange("p a b -> p (a b)"), bank_c(C_Y)[:, :],
                                x2b[:, :, :].rearrange("p a b -> p (a b)"), ALU.add).then_inc(c_evac, 1)

            def step(i):
                ahead, now, before, earlier = i + 1, i, i - 1, i - 2

                def do(n, fn, *k):
                    if on(n) and not (fn in (ln1_a, ln1_b) and known(n) and n == 0):
                        fn(n, *k)
                        later(split_weights, fn.__name__, n, *k)

                do(now, a_s, 1)
                do(before, b_qkv, 5)
                do(now, a_psum, 0)
                do(now, a_s, 2)
                do(now, a_s, 3)
                do(before, b_qkv, 6)
                do(now, a_psum, 1)
                do(now, a_pT, 0)
                do(now, a_pT, 1)
                do(ahead, ln1_a)
                do(before, b_qkv, 7)
                do(now, a_pv, 0)
                do(now, a_pT, 2)
                do(now, a_pT, 3)
                do(earlier, c_y)
                do(before, b_qkv, 8)
                do(before, b_qkv, 9)
                do(now, a_pv, 1)
                do(before, b_qkv, 10)
                do(ahead, ln1_b)
                do(before, b_qkv, 11)
                do(before, b_qkv, 12)
                do(now, a_y)
                do(now, ln2_a)
                do(ahead, a_cT)
                do(before, b_qkv, 13)
                do(before, b_qkv, 14)
                do(now, ln2_b)
                do(before, b_qkv, 15)
                do(now, b_xT, 0)
                do(now, b_xT, 1)
                do(ahead, a_xT)
                do(ahead, a_v)
                do(before, c_qk)
                do(now, b_route)
                do(before, c_s)
                do(ahead, a_kT)
                do(ahead, a_q, 0)
                do(before, c_p)
                do(ahead, a_q, 1)
                do(ahead, a_s, 0)
                do(now, b_wsum)
                do(before, c_pT)
                do(now, b_qkv, 0)
                do(now, b_qkv, 1)
                do(now, b_qkv, 2)
                do(before, c_mix, 0)
                do(before, c_mix, 1)
                do(now, b_qkv, 3)
                do(before, c_mix, 2)
                do(now, b_qkv, 4)
                do(before, c_mix, 3)

            dve.wait_ge(small_in, 48)
            V.tensor_tensor(sim_sq[:, :, :], sim_raw[:, :, :], sim_raw[:, :, :], ALU.mult).then_inc(sim_step, 1)
            ln1_a(0)
            dve.wait_ge(sim_norm, 1)
            V.tensor_copy(sim_n[:, :], bank_b(0)[:, 0:E]).then_inc(sim_norm, 1)
            ln1_b(0)
            split_weights(0)
            dve.wait_ge(sim_norm, 3)
            V.tensor_scalar(sim_n[:, :], sim_n[:, :], TINY, None, ALU.max).then_inc(sim_norm, 1)
            dve.wait_ge(sim_norm, 4)
            V.reciprocal(sim_n[:, :], sim_n[:, :]).then_inc(sim_step, 1)
            dve.wait_ge(sim_step, 2)
            V.tensor_tensor(sim_sq[:, :, :], sim_raw[:, :, :], sim_n[:, :].unsqueeze(1).to_broadcast([P, CC, E]),
                            ALU.mult).then_inc(sim_step, 1)
            dve.wait_ge(sim_step, 3)
            V.tensor_copy(wsim[0][:, :, :], sim_sq[:, :, :]).then_inc(sim_step, 1)
            dve.wait_ge(sim_step, 4)
            V.tensor_tensor(wsim[1][:, :, :], sim_sq[:, :, :], wsim[0].bitcast(F32)[:, :, :], ALU.subtract).then_inc(sim_step, 1)
            dve.wait_ge(sig_step, 1)
            V.tensor_scalar(half_e[:, :], half_e[:, :], 1.0, None, ALU.add).then_inc(sig_step, 1)
            dve.wait_ge(sig_step, 2)
            V.reciprocal(sig[:, :], half_e[:, :]).then_inc(sig_step, 1)
            for k in range(1, EARLY):
                split_weights(k)

            for i in range(-1, 3):
                step(i)
            with dve.Fori(3, B - 2) as i:
                step(i)
            for i in range(B - 2, B + 2):
                step(i)

        @block.gpsimd
        def _(pool):
            G = nc.gpsimd
            CHAIN = 10

            G.memset(ident[:, :], 0.0).then_inc(pool_step, 1)
            G.memset(causal[:, :], 0.0).then_inc(pool_step, 1)
            G.iota(iota_i[:, :], pattern=[[1, E]], base=0, channel_multiplier=0).then_inc(pool_step, 1)
            pool.wait_ge(pool_step, 3)
            G.affine_select(out=ident[:, :], in_=ident[:, :], compare_op=ALU.not_equal, fill=1.0, base=0,
                            pattern=[[-1, P]], channel_multiplier=1).then_inc(consts, 1)
            G.affine_select(out=causal[:, :], in_=causal[:, :], compare_op=ALU.is_ge, fill=MASKED, base=P,
                            pattern=[[-1, T]], channel_multiplier=1).then_inc(pool_step, 1)
            G.tensor_copy(iota[:, :], iota_i[:, :]).then_inc(pool_step, 1)
            pool.wait_ge(pool_step, 5)
            pool.wait_ge(consts, 4)
            START = 5

            def chain(n, which):
                return CHAIN * n + which + 1 + START

            def power(n, k):
                pool.wait_ge(ln_var[k], at(k + 1, n, k))
                m = (k + 1) * NT
                src = pow_in[k][:, :, :].rearrange("p a b -> p (a b)")[:, 0:m]
                dst = pow_out[k][:, :, :].rearrange("p a b -> p (a b)")[:, 0:m]
                if not (known(n) and n == 0):
                    pool.wait_ge(ln_done[k], at(NT, n - 1, NT - 1))
                    if k == 1:
                        pool.wait_ge(rn_step, at(3, n - 1, 0))
                G.tensor_tensor(dst, src, expo[:, 0:m], ALU.pow).then_inc(ln_pow[k], 1)

            def a_xb(n):
                pool.wait_ge(x_in, 16 * (n + 1))
                if known(n) and n == 0:
                    pool.wait_ge(small_in, 48)
                else:
                    pool.wait_ge(a_evac, a_read(n - 1, A_Y))
                G.tensor_tensor(xb[:, :, :], xt[:, :, :], bo_all[:, :].unsqueeze(1).to_broadcast([P, NT, C]),
                                ALU.add).then_inc(xb_ready, 1)

            def x2_move(n):
                pool.wait_ge(a_evac, a_read(n, A_Y))
                if not (known(n) and n == 0):
                    pool.wait_ge(c_evac, c_read(n - 1, C_Y))
                apart(pool)
                G.tensor_copy(x2b[:, :, :], x2a[:, :, :]).then_inc(x2_moved, 1)

            def b_route_1(n):
                pool.wait_ge(idx_ready, at(3, n, 2))
                apart(pool)
                G.tensor_scalar(z_top[:, :], top[:, :, 0], 0.0, None, ALU.max).then_inc(pool_step, 1)
                G.tensor_scalar(idle[:, :], top[:, :, 0], 0.0, None, ALU.is_le).then_inc(pool_step, 1)
                G.tensor_scalar(g[:, :, :], z[:, :, :], 0.0, None, ALU.max).then_inc(pool_step, 1)
                G.tensor_scalar(act_on[:, :, :], z[:, :, :], 0.0, None, ALU.is_gt).then_inc(pool_step, 1)
                pool.wait_ge(pool_step, chain(n, 3))
                G.tensor_tensor(g[:, :, :], g[:, :, :], z_top[:, :].unsqueeze(2).to_broadcast([P, NT, E]),
                                ALU.subtract).then_inc(g_ready, 1)

            def b_route_2(n):
                for t in range(NT):
                    G.tensor_scalar(first[:, t, :], iota[:, :], idxf[:, t, 0:1], idle[:, t:t + 1],
                                    ALU.is_equal, ALU.mult).then_inc(pool_step, 1)
                    G.tensor_scalar(second[:, t, :], iota[:, :], idxf[:, t, 1:2], idle[:, t:t + 1],
                                    ALU.is_equal, ALU.mult).then_inc(pool_step, 1)
                pool.wait_ge(pool_step, chain(n, 7))
                G.tensor_tensor(first[:, :, :], first[:, :, :], second[:, :, :], ALU.add).then_inc(pool_step, 1)
                pool.wait_ge(pool_step, chain(n, 8))
                G.tensor_tensor(act_on[:, :, :], act_on[:, :, :], first[:, :, :], ALU.add).then_inc(pool_step, 1)

            def b_w(n):
                pool.wait_ge(pool_step, chain(n, 9))
                pool.wait_ge(e_ready, at(1, n, 0))
                G.tensor_tensor(w[:, :, :], w[:, :, :], act_on[:, :, :], ALU.mult).then_inc(w_ready, 1)

            def b_rw(n):
                pool.wait_ge(w_sum_ready, at(2, n, 1))
                if not (known(n) and n == 0):
                    pool.wait_ge(c_fill, c_at(n - 1, C_RT))
                G.tensor_tensor(rw[:, :, :], w[:, :, :], w_sum[:, 1, :].unsqueeze(2).to_broadcast([P, NT, E]),
                                ALU.mult).then_inc(rw_ready, 1)

            def b_sum(n, t):
                pool.wait_ge(b_evac, b_read(n, B_QKV + NT * (EP - 1) + t))
                if not (known(n) and n == 0):
                    pool.wait_ge(v2_ready, at(2, n - 1, 1))
                    pool.wait_ge(c_fill, c_at(n - 1, C_QK))
                G.tensor_tensor(qkv[:, t, :], acc[:, t, 0, :], acc[:, t, 1, :], ALU.add).then_inc(qkv_ready, 1)

            def c_v(n):
                pool.wait_ge(qkv_ready, at(NT, n, NT - 1))
                if not (known(n) and n == 0):
                    pool.wait_ge(c_fill, c_at(n - 1, C_PV))
                apart(pool)
                v_in = qkv[:, :, 2 * D:QKV].unsqueeze(2).to_broadcast([P, NT, 2, D])
                G.tensor_copy(v2[0][:, :, :, :], v_in).then_inc(v2_ready, 1)
                pool.wait_ge(v2_ready, at(2, n, 0))
                G.tensor_tensor(v2[1][:, :, :, :], v_in, v2[0].bitcast(F32)[:, :, :, :], ALU.subtract).then_inc(v2_ready, 1)

            def a_p(n, half):
                pool.wait_ge(p_sum_ready, at(4, n, 2 * half + 1))
                part = probs[:, :, half * HB:(half + 1) * HB, :]
                G.tensor_tensor(part, part, p_sum[:, half, 1, :, :].unsqueeze(3).to_broadcast([P, NT, HB, NC]),
                                ALU.mult).then_inc(p_ready, 1)

            def c_mix(n, j):
                pool.wait_ge(mix_hi, at(4, n, j))
                G.tensor_tensor(mixs[1][:, 2 * j:2 * j + 2, :], mix[:, 2 * j:2 * j + 2, :],
                                mixs[0].bitcast(F32)[:, 2 * j:2 * j + 2, :], ALU.subtract).then_inc(mix_lo, 1)

            def step(i):
                ahead, now, before, earlier = i + 1, i, i - 1, i - 2

                def do(n, fn, *k):
                    if on(n):
                        fn(n, *k)

                do(earlier, c_mix, 1)
                do(earlier, c_mix, 2)
                do(earlier, c_mix, 3)
                do(now, a_p, 0)
                do(now, a_p, 1)
                if not (known(ahead) and ahead == 0):
                    do(ahead, power, 0)
                do(before, x2_move)
                do(now, power, 1)
                do(before, b_sum, 0)
                do(before, b_sum, 1)
                do(before, c_v)
                do(now, b_route_1)
                do(now, b_route_2)
                do(now, b_w)
                do(now, b_rw)
                do(ahead, a_xb)
                do(before, c_mix, 0)

            power(0, 0)
            pool.wait_ge(sim_norm, 2)
            G.tensor_tensor(sim_n[:, :], sim_n[:, :], expo[:, NT:NT + 1].to_broadcast([P, E]), ALU.pow).then_inc(sim_norm, 1)

            for i in range(-1, 3):
                step(i)
            with pool.Fori(3, B - 2) as i:
                step(i)
            for i in range(B - 2, B + 2):
                step(i)


_INS = ['x', 'ctx_768', 'L0_xattn_Wq', 'L0_xattn_Wk', 'L0_xattn_Wv', 'L0_xattn_Wo', 'L0_xattn_bo', 'L0_ffn_sim_matrix',
        'L0_ffn_gates', 'L0_ffn_q_proj', 'L0_ffn_k_proj', 'L0_ffn_v_proj', 'L0_ffn_o_proj']


def kernel(**inputs):
    import numpy as _np
    import concourse.bacc as _bacc
    from concourse import mybir as _mybir
    from concourse.bass_utils import run_bass_kernel_spmd as _run

    nc = _bacc.Bacc("TRN2", target_bir_lowering=False, num_devices=1)
    arrays, args = {}, []
    for name in _INS:
        a = _np.ascontiguousarray(inputs[name])
        arrays[f"in_{name}_dram"] = a
        args.append(nc.dram_tensor(f"in_{name}_dram", a.shape, _mybir.dt.from_np(a.dtype), kind="ExternalInput").ap())
    shape = inputs['x'].shape
    args.append(nc.dram_tensor("out_0_dram", shape, _mybir.dt.float32, kind="ExternalOutput").ap())
    experts, tokens = inputs['L0_ffn_gates'].shape[0], shape[1]
    args.append(nc.dram_tensor("rw_dram", (experts, tokens), _mybir.dt.float32, kind="Internal").ap())
    xattn_moe_kernel(nc, *args)
    r = _run(nc, [arrays], core_ids=[0])
    return r.results[0]["out_0_dram"]
```
